# Optimizing a Trainium2 kernel written in Bass

```python
import numpy as np
import jax
import jax.numpy as jnp

def _softmax(x, axis=-1):
    return jax.nn.softmax(x, axis=axis)

def _gelu(x):
    return jax.nn.gelu(x, approximate=True)

def _silu(x):
    return jax.nn.silu(x)

def _sigmoid(x):
    return jax.nn.sigmoid(x)

def _layernorm(x, axis=-1, eps=1e-05):
    m = jnp.mean(x, axis=axis, keepdims=True)
    v = jnp.var(x, axis=axis, keepdims=True)
    return (x - m) / jnp.sqrt(v + eps)

def _scatter_add(tgt, idx, src, axis=0):
    return tgt.at[idx].add(src)

def _segment_sum(src, seg, n):
    return jax.ops.segment_sum(src, seg, n)
kernel_name = 'mk_gnn_preln_d2_gnn_r8_dd2f54'

def setup_inputs(seed: int=0):
    np.random.seed(seed)
    _w = jnp.asarray

    def _rec_inputs():
        import jax
        import jax.numpy as jnp
        _gk = jax.random.key(seed)
        x = -0.0003713 + 1 * jax.random.normal(jax.random.fold_in(_gk, 1), (12500, 128), jnp.float32)
        _s = jax.random.randint(jax.random.fold_in(_gk, 2), (100000,), 0, 12500, jnp.int32)
        _d = jax.random.randint(jax.random.fold_in(_gk, 3), (100000,), 0, 12500, jnp.int32)
        _loop = jnp.arange(12500, dtype=jnp.int32)
        src = jnp.concatenate([_s, _d, _loop])
        dst = jnp.concatenate([_d, _s, _loop])
        _o = jnp.argsort(dst, stable=True)
        src = src[_o]
        dst = dst[_o]
        return (x, src, dst)
    x, src, dst = _rec_inputs()

    def _L0_gnn_setup():
        import jax, jax.numpy as jnp
        import numpy as np
        N_NODES = 12500
        N_EDGES = 200000
        F_IN = 128
        F_OUT = 128
        key = jax.random.key(seed)
        k1, k2, k3, k4, k5 = jax.random.split(key, 5)
        features = jax.random.normal(k1, (N_NODES, F_IN), dtype=jnp.float32)
        scale = float(np.sqrt(2.0 / (F_IN + F_OUT)))
        w_s = jax.random.normal(k2, (F_IN, F_OUT), dtype=jnp.float32) * scale
        w_n = jax.random.normal(k3, (F_IN, F_OUT), dtype=jnp.float32) * scale
        src = jax.random.randint(k4, (N_EDGES,), 0, N_NODES, dtype=jnp.int32)
        dst = jax.random.randint(k5, (N_EDGES,), 0, N_NODES, dtype=jnp.int32)
        return {'features': features, 'w_s': w_s, 'w_n': w_n, 'src': src, 'dst': dst}
    _L0_gnn_all = _L0_gnn_setup()
    _L0_gnn_in = {k: v for k, v in _L0_gnn_all.items() if k in ('w_s', 'w_n')}
    del _L0_gnn_all

    def _L1_gnn_setup():
        import jax, jax.numpy as jnp
        import numpy as np
        N_NODES = 6250
        N_EDGES = 100000
        DIM = 128
        BN_EPS = 1e-05
        key = jax.random.key(seed)
        ks = jax.random.split(key, 12)
        d = DIM
        s = 1.0 / np.sqrt(d)
        x = jax.random.normal(ks[0], (N_NODES, d), dtype=jnp.float32)
        edge_index = jax.random.randint(ks[1], (2, N_EDGES), 0, N_NODES, dtype=jnp.int64)
        W_msg = jax.random.uniform(ks[2], (d, d), jnp.float32, -s, s)
        b_msg = jax.random.uniform(ks[3], (d,), jnp.float32, -s, s)
        sa = 1.0 / np.sqrt(2 * d)
        W_att = jax.random.uniform(ks[4], (2 * d, 1), jnp.float32, -sa, sa)
        b_att = jax.random.uniform(ks[5], (1,), jnp.float32, -sa, sa)
        W_ih = jax.random.uniform(ks[6], (3 * d, d), jnp.float32, -s, s)
        b_ih = jax.random.uniform(ks[7], (3 * d,), jnp.float32, -s, s)
        W_hh = jax.random.uniform(ks[8], (3 * d, d), jnp.float32, -s, s)
        b_hh = jax.random.uniform(ks[9], (3 * d,), jnp.float32, -s, s)
        gamma = jnp.ones((d,), jnp.float32)
        beta = jnp.zeros((d,), jnp.float32)
        return {'x': x, 'edge_index': edge_index, 'W_msg': W_msg, 'b_msg': b_msg, 'W_att': W_att, 'b_att': b_att, 'W_ih': W_ih, 'b_ih': b_ih, 'W_hh': W_hh, 'b_hh': b_hh, 'gamma': gamma, 'beta': beta}
    _L1_gnn_all = _L1_gnn_setup()
    _L1_gnn_in = {k: v for k, v in _L1_gnn_all.items() if k in ('W_msg', 'b_msg', 'W_att', 'b_att', 'W_ih', 'b_ih', 'W_hh', 'b_hh', 'gamma', 'beta')}
    del _L1_gnn_all
    return {'x': x, 'src': src, 'dst': dst, 'L0_gnn_w_s': _L0_gnn_in['w_s'], 'L0_gnn_w_n': _L0_gnn_in['w_n'], 'L1_gnn_W_msg': _L1_gnn_in['W_msg'], 'L1_gnn_b_msg': _L1_gnn_in['b_msg'], 'L1_gnn_W_att': _L1_gnn_in['W_att'], 'L1_gnn_b_att': _L1_gnn_in['b_att'], 'L1_gnn_W_ih': _L1_gnn_in['W_ih'], 'L1_gnn_b_ih': _L1_gnn_in['b_ih'], 'L1_gnn_W_hh': _L1_gnn_in['W_hh'], 'L1_gnn_b_hh': _L1_gnn_in['b_hh'], 'L1_gnn_gamma': _L1_gnn_in['gamma'], 'L1_gnn_beta': _L1_gnn_in['beta']}

def reference(x, src, dst, L0_gnn_w_s, L0_gnn_w_n, L1_gnn_W_msg, L1_gnn_b_msg, L1_gnn_W_att, L1_gnn_b_att, L1_gnn_W_ih, L1_gnn_b_ih, L1_gnn_W_hh, L1_gnn_b_hh, L1_gnn_gamma, L1_gnn_beta):
    import jax
    import jax.numpy as jnp

    def _L0_gnn_ref(features, w_s, w_n, src, dst):
        import jax, jax.numpy as jnp
        import numpy as np
        N_NODES = 12500
        N_EDGES = 200000
        F_IN = 128
        F_OUT = 128
        self_conv = features @ w_s
        nbr_conv = features @ w_n
        messages = nbr_conv[src]
        n = features.shape[0]
        agg = jax.ops.segment_sum(messages, dst, num_segments=n)
        return jax.nn.relu(self_conv + agg)

    def _L1_gnn_ref(x, edge_index, W_msg, b_msg, W_att, b_att, W_ih, b_ih, W_hh, b_hh, gamma, beta):
        import jax, jax.numpy as jnp
        import numpy as np
        N_NODES = 6250
        N_EDGES = 100000
        DIM = 128
        BN_EPS = 1e-05
        num_nodes, d = x.shape
        src = edge_index[0]
        dst = edge_index[1]
        xs = x[src]
        xd = x[dst]
        att = jax.nn.sigmoid(xs @ W_att[:d] + xd @ W_att[d:] + b_att)
        messages = (xs @ W_msg + b_msg) * att
        aggregated = jax.ops.segment_sum(messages, dst, num_segments=num_nodes)
        gi = aggregated @ W_ih.T + b_ih
        gh = x @ W_hh.T + b_hh
        i_r, i_z, i_n = jnp.split(gi, 3, axis=1)
        h_r, h_z, h_n = jnp.split(gh, 3, axis=1)
        r = jax.nn.sigmoid(i_r + h_r)
        z = jax.nn.sigmoid(i_z + h_z)
        n = jnp.tanh(i_n + r * h_n)
        h_new = (1.0 - z) * n + z * x
        mean = jnp.mean(h_new, axis=0)
        var = jnp.var(h_new, axis=0)
        return gamma * (h_new - mean) * jax.lax.rsqrt(var + BN_EPS) + beta
    edge_index = jnp.stack([src, dst])
    h = jnp.maximum(_layernorm(x, axis=-1), 0.0)
    x = x + _L0_gnn_ref(h, L0_gnn_w_s, L0_gnn_w_n, src, dst)
    h = jnp.maximum(_layernorm(x, axis=-1), 0.0)
    x = x + _L1_gnn_ref(h, edge_index, L1_gnn_W_msg, L1_gnn_b_msg, L1_gnn_W_att, L1_gnn_b_att, L1_gnn_W_ih, L1_gnn_b_ih, L1_gnn_W_hh, L1_gnn_b_hh, L1_gnn_gamma, L1_gnn_beta)
    return x

_drawn_inputs = setup_inputs


def setup_inputs(seed=0):
    import zlib

    import numpy as np

    out = dict(_drawn_inputs(seed))
    spreads = {'L1_gnn_gamma': (1.0, 0.2), 'L1_gnn_beta': (0.0, 0.369)}
    factors = {'L1_gnn_b_ih': 8.0, 'L1_gnn_b_hh': 8.0}
    for name, (base, spread) in spreads.items():
        noise = np.random.default_rng([zlib.crc32(name.encode()), seed]).standard_normal(out[name].shape)
        drawn = base * np.exp(spread * noise) if base else spread * noise
        out[name] = jnp.asarray(drawn.astype(out[name].dtype))
    for name, factor in factors.items():
        out[name] = (out[name] * factor).astype(out[name].dtype)
    return out
```

```python
from contextlib import ExitStack

import concourse.bass as bass
from concourse import mybir

P = 128
D = 128
TPB = 17
STRIDE = 8
MARGIN = 64
ROW1 = 144
LN_EPS = 1e-5
BN_EPS = 1e-5
OFF = float(1 << 20)
GROUPS = ((0, 4), (4, 8), (8, 12), (12, TPB))
STEP_EDGES = TPB * P

ALU = mybir.AluOpType
ACT = mybir.ActivationFunctionType
AX = mybir.AxisListType
F32 = mybir.dt.float32
I32 = mybir.dt.int32


def pairs(eng, count, body, last_apart=False):
    turns = count // 2
    end = turns - 1 if last_apart and turns > 1 else turns
    body(0, 0, True)
    body(1, 1, True)
    if end > 1:
        with eng.Fori(1, end, 1) as turn:
            body(turn * 2, 0, False)
            body(turn * 2 + 1, 1, False)
    if end < turns:
        body(count - 2, 0, False)
        body(count - 1, 1, False)


def gnn_program(nc, x, src, dst, w_s, w_n, w_msg, b_msg, w_att, b_att, w_ih, b_ih, w_hh, b_hh,
                gamma, beta, out):
    N = x.shape[0]
    E = src.shape[0]
    NB = -(-N // P)
    assert NB % 2 == 0 and -(-E // STEP_EDGES) == NB and STRIDE * TPB >= P
    TAIL = N - (NB - 1) * P
    EFULL = E // STEP_EDGES
    ETAIL = E - EFULL * STEP_EDGES
    COLS = MARGIN + NB * P + MARGIN
    LB = 7 if NB % 14 == 0 else NB // 2
    NCH = NB // LB
    TILES = NB * TPB
    TURNS = -(-TPB // 4)
    WIN = STRIDE * (TPB - 1) + P
    PAD0 = EFULL // 32 * 32
    EDGE_DMAS = 2 * ((PAD0 > 0) + EFULL - PAD0 + (ETAIL > 0))

    h0_table = nc.dram_tensor("h0_table", [NB * P, D], F32, kind="Internal").ap()
    msg_table = nc.dram_tensor("msg_table", [NB * P, ROW1], F32, kind="Internal").ap()
    x1_rows = nc.dram_tensor("x1_rows", [NB * P, D], F32, kind="Internal").ap()
    h1t_blocks = nc.dram_tensor("h1t_blocks", [NB, D, P], F32, kind="Internal").ap()

    ctx = ExitStack()
    with ctx:
        def sb(name, shape, dt=F32):
            return ctx.enter_context(nc.sbuf_tensor(name, shape, dt))

        def sem(name):
            return ctx.enter_context(nc.semaphore(name))

        agg = sb("agg", [P, COLS])
        adx = sb("adx", [P, COLS])
        srcT = sb("srcT", [P, NB + 2, TPB], I32)
        dstT = sb("dstT", [P, NB, TPB])
        idx = sb("idx", [P, 2, TPB], I32)
        rows = sb("rows", [P, 2, TPB, ROW1])
        win = sb("win", [P, TPB, P])
        select = sb("select", [P, 2, TPB, P])
        gate = sb("gate", [P, TPB, P])
        ident = sb("ident", [P, P])
        ones = sb("ones", [P, P])
        zeros = sb("zeros", [P, P])
        weight_s = sb("weight_s", [D, D])
        weight_n = sb("weight_n", [D, D])
        weight_m = sb("weight_m", [D, D + 1])
        att_d = sb("att_d", [D, 1])
        att_d_all = sb("att_d_all", [D, P])
        w_in = sb("w_in", [P, 6, D])
        w_gates = sb("w_gates", [D, 6, P])
        b_row = sb("b_row", [1, D + 1])
        b_all = sb("b_all", [P, D + 1])
        b_msg_all = sb("b_msg_all", [P, D + 1])
        b_cols = sb("b_cols", [P, 8])
        b_rz = sb("b_rz", [P, 2])
        eps = sb("eps", [P, 1])
        jbase = sb("jbase", [P, TPB])
        jbase_i = sb("jbase_i", [P, TPB], I32)
        rowbase = sb("rowbase", [P, 1])
        rowbase_i = sb("rowbase_i", [P, 1], I32)
        blkbase = sb("blkbase", [P, NB])
        blkbase_i = sb("blkbase_i", [P, NB], I32)
        flags = sb("flags", [P, 8])
        bad_i = sb("bad_i", [1, 1], I32)
        gen_dst = sb("gen_dst", [P, 1])
        gen_src = sb("gen_src", [P, 1], I32)
        st = sb("st", [P, 2, LB, 6])
        ln = sb("ln", [P, 2, 8, LB])
        h0b = sb("h0b", [P, 2, D])
        h0T = sb("h0T", [D, 2, P])
        aggs = sb("aggs", [D, 2, P])
        x1b = sb("x1b", [P, 2, D])
        hnb = sb("hnb", [P, 2, D])
        h1T = sb("h1T", [D, 2, P])
        msgb = sb("msgb", [P, 2, ROW1])
        nst = sb("nst", [P, 2, 12])
        rz = sb("rz", [P, 2, P])
        tmp = sb("tmp", [P, 4, P])
        bst = sb("bst", [P, NB, 6])
        bn = sb("bn", [P, 8])

        STAGED = 4 * STEP_EDGES + 2 * LB * D
        stage = agg if COLS >= STAGED else sb("stage", [P, STAGED])
        e_src_i = stage[:, 0:STEP_EDGES].bitcast(I32)
        e_dst_i = stage[:, STEP_EDGES:2 * STEP_EDGES].bitcast(I32)
        e_src = stage[:, 2 * STEP_EDGES:3 * STEP_EDGES]
        e_dst = stage[:, 3 * STEP_EDGES:4 * STEP_EDGES]
        h0s = stage[:, 4 * STEP_EDGES:STAGED].rearrange("p (c b f) -> p c b f", c=2, f=D)
        y_s = select[:, :, 0:LB, :]
        out_s = rows[:, :, :, :].rearrange("p a t r -> p a (t r)")[:, :, 0:LB * D].rearrange(
            "p a (b f) -> p a b f", f=D)

        ps = ctx.enter_context(nc.psum_tensor("ps", [P, 8, 512], F32))
        ps_agg = ps[:, 0:2, 0:WIN]
        ps_t = ps[:, 2, :]
        ps_c = ps[:, 3, :]
        ps_m = ps[:, 4, :]
        ps_g = ps[:, 5, 0:P]
        ps_a = ps[:, 6, 0:P]
        ps_w = ps[:, 6, :]
        ps_h = ps[:, 7, 0:P]
        ps_y = [ps[:, 2 * c:2 * c + 2, :].rearrange("p a b -> p (a b)")[:, 0:LB * D] for c in range(2)]

        def block_cols(k, w=P):
            return bass.ds(k * P + MARGIN, w)

        edges_in = sem("edges_in")
        weights_in = sem("weights_in")
        x_in = [sem(f"x_in{c}") for c in range(2)]
        h0_out = [sem(f"h0_out{c}") for c in range(2)]
        gathered = [sem(f"gathered{s}") for s in range(2 * TPB)]
        gen_gathered = sem("gen_gathered")
        h0_in = [sem(f"h0_in{c}") for c in range(2)]
        x1_out = [sem(f"x1_out{c}") for c in range(2)]
        msg_out = [sem(f"msg_out{c}") for c in range(2)]
        h1t_out = [sem(f"h1t_out{c}") for c in range(2)]
        h1t_in = [sem(f"h1t_in{c}") for c in range(2)]
        x1_in = [sem(f"x1_in{c}") for c in range(2)]
        y_out = [sem(f"y_out{c}") for c in range(2)]
        pads_set = sem("pads_set")
        zero_set = sem("zero_set")
        consts = sem("consts")
        setup_dve = sem("setup_dve")
        flag_sum = sem("flag_sum")
        flag_ready = sem("flag_ready")
        edges_turned = sem("edges_turned")
        edges_kept = sem("edges_kept")
        weights_turned = sem("weights_turned")
        biases_spread = sem("biases_spread")
        weights_ready = sem("weights_ready")
        agg_zeroed = sem("agg_zeroed")
        ln_stats = sem("ln_stats")
        ln_var = sem("ln_var")
        ln_std = sem("ln_std")
        ln_rstd = sem("ln_rstd")
        ln_ready = sem("ln_ready")
        ln_done = sem("ln_done")
        own_waits = sem("own_waits")
        gen_idx = sem("gen_idx")
        gen_sig = sem("gen_sig")
        gen_sel = sem("gen_sel")
        gen_next = sem("gen_next")
        gen_mm = sem("gen_mm")
        gen_add = sem("gen_add")
        idx_ready = sem("idx_ready")
        sel_ready = sem("sel_ready")
        sums_ready = [sem(f"sums_ready{n}") for n in range(2)]
        sums_added = [sem(f"sums_added{n}") for n in range(2)]
        gate_ready = [sem(f"gate_ready{g}") for g in range(len(GROUPS))]
        att_ready = [sem(f"att_ready{g}") for g in range(len(GROUPS))]
        n0_turned = sem("n0_turned")
        n0_h0T = sem("n0_h0T")
        n0_agg = sem("n0_agg")
        n0_conv = sem("n0_conv")
        n0_x1 = sem("n0_x1")
        n0_stats = sem("n0_stats")
        n0_var = sem("n0_var")
        n0_std = sem("n0_std")
        n0_rstd = sem("n0_rstd")
        n0_norm = sem("n0_norm")
        n0_hT = sem("n0_hT")
        n0_h1T = sem("n0_h1T")
        n0_proj = sem("n0_proj")
        n0_msg = sem("n0_msg")
        n0_ad = sem("n0_ad")
        n1_gates = sem("n1_gates")
        n1_rz = sem("n1_rz")
        n1_rh = sem("n1_rh")
        n1_pre = sem("n1_pre")
        n1_cand = sem("n1_cand")
        n1_diff = sem("n1_diff")
        n1_zd = sem("n1_zd")
        n1_hnew = sem("n1_hnew")
        n1_bst = sem("n1_bst")
        bn_dve = sem("bn_dve")
        bn_std = sem("bn_std")
        y_scaled = sem("y_scaled")
        y_turned = sem("y_turned")
        y_added = sem("y_added")

        block = ctx.enter_context(nc.Block())

        @block.sync
        def _(sp):
            main = PAD0
            views = [(e_src_i, src), (e_dst_i, dst)]
            if main:
                for to, of in views:
                    sp.dma_start(to[0:main, :], of[0:main * STEP_EDGES].rearrange(
                        "(p n) -> p n", n=STEP_EDGES)).then_inc(edges_in, 16)
            sp.wait_ge(pads_set, 1)
            for to, of in views:
                for q in range(main, EFULL + (ETAIL > 0)):
                    n = STEP_EDGES if q < EFULL else ETAIL
                    sp.dma_start(to[q:q + 1, 0:n], of[q * STEP_EDGES:q * STEP_EDGES + n].rearrange(
                        "(p n) -> p n", p=1)).then_inc(edges_in, 16)

            def load_x(c, par, first):
                if not first:
                    sp.wait_ge(x_in[par], (c - par) * 8)
                last = isinstance(c, int) and c == NCH - 1
                full = LB - 1 if last else LB
                if full:
                    sp.dma_start(
                        adx[:, bass.ds(c * (LB * D) + MARGIN, full * D)].rearrange("p (b f) -> p b f", f=D),
                        x[bass.ds(c * (LB * P), full * P), :].rearrange("(b p) f -> p b f", p=P),
                    ).then_inc(x_in[par], 16)
                if last:
                    sp.dma_start(adx[0:TAIL, MARGIN + (NB - 1) * D:MARGIN + NB * D],
                                 x[(NB - 1) * P:N, :]).then_inc(x_in[par], 16)

            def store_h0(c, par, first):
                sp.wait_ge(ln_done, c + 1)
                sp.dma_start(h0_table[bass.ds(c * (LB * P), LB * P), :].rearrange("(b p) f -> p b f", p=P),
                             h0s[:, par]).then_inc(h0_out[par], 16)

            def chunk(c, par, first):
                load_x(c, par, first)
                if not first:
                    store_h0(c - 2, par, False)

            chunk(0, 0, True)
            chunk(1, 1, True)
            for to, of in ((weight_s[:], w_s), (weight_n[:], w_n), (weight_m[:, 0:D], w_msg),
                           (weight_m[:, D:D + 1], w_att[0:D, :]), (att_d[:], w_att[D:2 * D, :]),
                           (w_in[:, 0:3, :], w_ih.rearrange("(g p) d -> p g d", p=P)),
                           (w_in[:, 3:6, :], w_hh.rearrange("(g p) d -> p g d", p=P)),
                           (b_row[:, 0:D], b_msg.rearrange("(a d) -> a d", a=1)),
                           (b_row[:, D:D + 1], b_att.rearrange("(a d) -> a d", a=1)),
                           (b_cols[:, 0:3], b_ih.rearrange("(g p) -> p g", p=P)),
                           (b_cols[:, 3:6], b_hh.rearrange("(g p) -> p g", p=P)),
                           (b_cols[:, 6:7], gamma.rearrange("(p a) -> p a", a=1)),
                           (b_cols[:, 7:8], beta.rearrange("(p a) -> p a", a=1))):
                sp.dma_start(to, of, allow_slow_non_contiguous=True).then_inc(weights_in, 16)
            if NCH > 2:
                if NCH > 4:
                    with sp.Fori(1, NCH // 2 - 1, 1) as turn:
                        chunk(turn * 2, 0, False)
                        chunk(turn * 2 + 1, 1, False)
                chunk(NCH - 2, 0, False)
                chunk(NCH - 1, 1, False)
            store_h0(NCH - 2, 0, False)
            store_h0(NCH - 1, 1, False)

            for c in range(2):
                sp.wait_ge(h0_out[c], 16 * (NCH // 2))

            def load_h0(k, par):
                sp.dma_start(h0b[:, par], h0_table[bass.ds(k * P, P), :]).then_inc(h0_in[par], 16)

            load_h0(0, 0)
            load_h0(1, 1)

            def nodes0(k, par, first):
                last = isinstance(k, int) and k >= NB - 2
                if not last:
                    sp.wait_ge(n0_turned, k + 1)
                    load_h0(k + 2, par)
                sp.wait_ge(n0_x1, k + 1)
                sp.dma_start(x1_rows[bass.ds(k * P, P), :], x1b[:, par]).then_inc(x1_out[par], 16)
                sp.wait_ge(n0_h1T, k + 1)
                sp.dma_start(h1t_blocks[bass.ds(k, 1)].rearrange("a f n -> f (a n)"),
                             h1T[:, par]).then_inc(h1t_out[par], 16)
                sp.wait_ge(n0_msg, k + 1)
                sp.dma_start(msg_table[bass.ds(k * P, P), :], msgb[:, par]).then_inc(msg_out[par], 16)

            pairs(sp, NB, nodes0, last_apart=True)
            for c in range(2):
                sp.wait_ge(x1_out[c], 16 * (NB // 2))
                sp.wait_ge(h1t_out[c], 16 * (NB // 2))

            def load_h1(k, par):
                sp.dma_start(h1T[:, par], h1t_blocks[bass.ds(k, 1)].rearrange("a f n -> f (a n)")
                             ).then_inc(h1t_in[par], 16)

            load_h1(0, 0)
            load_h1(1, 1)

            def nodes1(k, par, first):
                last = isinstance(k, int) and k >= NB - 2
                if not last:
                    sp.wait_ge(n1_diff, k + 1)
                    load_h1(k + 2, par)
                sp.wait_ge(att_ready[-1], NB if last else k + 2)
                sp.dma_start(adx[:, block_cols(k)], x1_rows[bass.ds(k * P, P), :]).then_inc(x1_in[par], 16)

            pairs(sp, NB, nodes1, last_apart=True)

            def store_y(c, par, first):
                sp.wait_ge(y_added, c + 1)
                last = isinstance(c, int) and c == NCH - 1
                full = LB - 1 if last else LB
                if full:
                    sp.dma_start(out[bass.ds(c * (LB * P), full * P), :].rearrange("(b p) f -> p b f", p=P),
                                 out_s[:, par, 0:full, :]).then_inc(y_out[par], 16)
                if last:
                    sp.dma_start(out[(NB - 1) * P:N, :], out_s[0:TAIL, par, LB - 1, :]
                                 ).then_inc(y_out[par], 16)

            pairs(sp, NCH, store_y, last_apart=True)
            sp.wait_ge(y_out[0], 16 * (NCH // 2))
            sp.wait_ge(y_out[1], 16 * (NCH // 2 + (1 if LB > 1 else 0)))

        @block.gpsimd
        def _(pool):
            nc.gpsimd.memset(ident[:], 0.0).then_inc(zero_set, 1)
            pool.wait_ge(zero_set, 1)
            nc.gpsimd.affine_select(out=ident[:], in_=ident[:], compare_op=ALU.not_equal, fill=1.0, base=0,
                                    pattern=[[-1, P]], channel_multiplier=1).then_inc(consts, 1)
            nc.gpsimd.iota(rowbase_i[:], pattern=[[0, 1]], base=0, channel_multiplier=P).then_inc(consts, 1)
            nc.gpsimd.iota(jbase_i[:], pattern=[[STRIDE, TPB]], base=0, channel_multiplier=0).then_inc(consts, 1)
            nc.gpsimd.iota(select[:, 0].bitcast(I32), pattern=[[STRIDE, TPB], [1, P]], base=-MARGIN,
                           channel_multiplier=0).then_inc(consts, 1)
            nc.gpsimd.iota(blkbase_i[:], pattern=[[P, NB]], base=1 << 20, channel_multiplier=0
                           ).then_inc(consts, 1)
            pool.wait_ge(flag_ready, 1)
            bad = pool.value_load(bad_i[0:1, 0:1], min_val=0, max_val=1)

            for layer, (table, width) in enumerate(((h0_table, D), (msg_table, ROW1))):
                for c in range(2):
                    if layer == 0:
                        pool.wait_ge(h0_out[c], 16 * (NCH // 2))
                    else:
                        pool.wait_ge(msg_out[c], 16 * (NB // 2))
                with pool.If(bad):
                    with pool.Fori(0, TILES, 1) as t:
                        pool.wait_ge(gen_idx, t + (layer * TILES + 1)).then_inc(own_waits, 1)
                        pool.indirect_dma_start(
                            out=rows[:, 0, 0, 0:width], out_offset=None, in_=table,
                            in_offset=bass.IndirectOffsetOnAxis(ap=gen_src[:, 0:1], axis=0)
                        ).then_inc(gen_gathered, 16)
                    pool.wait_ge(gen_add, (layer + 1) * TILES * NB)
                    pool.nop()

                def gathers(i, par, first):
                    pool.wait_ge(idx_ready, i + (layer * NB + 1)).then_inc(own_waits, 1)
                    for j in range(TPB):
                        pool.indirect_dma_start(
                            out=rows[:, par, j, 0:width], out_offset=None, in_=table,
                            in_offset=bass.IndirectOffsetOnAxis(ap=idx[:, par, j:j + 1], axis=0)
                        ).then_inc(gathered[par * TPB + j], 16)

                pairs(pool, NB, gathers)

        @block.scalar
        def _(act):
            def norm(c, par, first):
                act.wait_ge(ln_var, c + 1)
                nc.scalar.activation(ln[:, par, 4], ln[:, par, 3], ACT.Sqrt, bias=eps[:, 0:1], scale=1.0 / D
                                     ).then_inc(ln_std, 1)
                act.wait_ge(ln_ready, c + 1)
                if not first:
                    act.wait_ge(h0_out[par], (c - par) * 8)
                for b in range(LB):
                    last = nc.scalar.activation(
                        h0s[:, par, b, :], adx[:, bass.ds(c * (LB * D) + (MARGIN + b * D), D)], ACT.Relu,
                        bias=ln[:, par, 6, b:b + 1], scale=ln[:, par, 5, b:b + 1])
                last.then_inc(ln_done, 1)

            act.wait_ge(pads_set, 1)
            pairs(act, NCH, norm)
            act.wait_ge(flag_ready, 1)
            bad = act.value_load(bad_i[0:1, 0:1], min_val=0, max_val=1)
            act.wait_ge(weights_ready, 1)

            def turned0(k, par):
                act.wait_ge(n0_turned, k + 1)
                nc.scalar.copy(h0T[:, par], ps_t[:, 0:P]).then_inc(n0_h0T, 1)
                act.wait_ge(sums_added[0], NB if isinstance(k, int) and k == NB - 1 else k + 2)
                nc.scalar.copy(aggs[:, par], agg[:, block_cols(k)]).then_inc(n0_agg, 1)

            def std0(k, par):
                act.wait_ge(n0_var, k + 1)
                nc.scalar.activation(nst[:, par, 8:9], nst[:, par, 7:8], ACT.Sqrt, bias=eps[:, 0:1]
                                     ).then_inc(n0_std, 1)

            def rest0(k, par, first):
                act.wait_ge(n0_hT, k + 1)
                if not first:
                    act.wait_ge(h1t_out[par], (k - par) * 8)
                nc.scalar.activation(h1T[:, par], ps_h, ACT.Relu).then_inc(n0_h1T, 1)
                act.wait_ge(n0_proj, k + 1)
                nc.scalar.activation(adx[:, block_cols(k)], ps_a, ACT.Identity,
                                     bias=b_all[:, D:D + 1]).then_inc(n0_ad, 1)

            def nodes0(k, par, first):
                turned0(k, par)
                std0(k, par)
                rest0(k, par, first)

            pairs(act, NB, nodes0, last_apart=True)
            act.wait_ge(n0_ad, NB)

            with act.If(bad):
                with act.Fori(0, TILES, 1) as t:
                    act.wait_ge(gen_gathered, t * 16 + 16 * (TILES + 1))
                    with act.Fori(0, NB, 1) as k:
                        act.wait_ge(gen_add, t * NB + (k + TILES * NB))
                        nc.scalar.activation(gate[:, 0], adx[:, block_cols(k)], ACT.Sigmoid,
                                             bias=rows[:, 0, 0, D:D + 1]).then_inc(gen_sig, 1)
                act.wait_ge(gen_add, 2 * TILES * NB)
                act.nop()

            def gates1(k, par):
                act.wait_ge(n1_gates, k + 1)
                if not (isinstance(k, int) and k == 0):
                    act.wait_ge(n1_zd, k)
                nc.scalar.activation(rz[:, 0], ps_c[:, 0:P], ACT.Sigmoid, bias=b_rz[:, 0:1])
                nc.scalar.activation(rz[:, 1], ps_c[:, P:2 * P], ACT.Sigmoid, bias=b_rz[:, 1:2]
                                     ).then_inc(n1_rz, 1)

            def cand1(k, par):
                act.wait_ge(n1_pre, k + 1)
                if not (isinstance(k, int) and k == 0):
                    act.wait_ge(n1_hnew, k)
                nc.scalar.activation(tmp[:, 2], tmp[:, 1], ACT.Tanh, bias=b_cols[:, 2:3]).then_inc(n1_cand, 1)

            def step1(i, par, first, tiles=True):
                for g, (j0, j1) in enumerate(GROUPS):
                    if tiles:
                        if g == 0 and not (isinstance(i, int) and i == 0):
                            act.wait_ge(att_ready[-1], i)
                        for j in range(j0, j1):
                            act.wait_ge(gathered[par * TPB + j],
                                        (i - par) * 8 + 16 * (NB // 2 + 1))
                            last = nc.scalar.activation(
                                gate[:, j], adx[:, bass.ds(i * P + STRIDE * j, P)], ACT.Sigmoid,
                                bias=rows[:, par, j, D:D + 1])
                        last.then_inc(gate_ready[g], 1)
                    if not first and g == 1:
                        gates1(i - 2, par)
                    if not first and g == 2:
                        cand1(i - 2, par)

            pairs(act, NB, step1)
            step1(NB, 0, False, False)
            step1(NB + 1, 1, False, False)

            act.wait_ge(bn_dve, 1)
            nc.scalar.activation(bn[:, 2:3], bn[:, 1:2], ACT.Sqrt, bias=eps[:, 0:1]).then_inc(bn_std, 1)
            act.wait_ge(bn_dve, 5)

            def scale(c, par, first):
                if not first:
                    act.wait_ge(y_turned, c - 1)
                nc.scalar.activation(y_s[:, par], agg[:, bass.ds(c * (LB * P) + MARGIN, LB * P)].rearrange(
                    "p (b n) -> p b n", n=P), ACT.Identity, bias=bn[:, 5:6], scale=bn[:, 4:5]
                ).then_inc(y_scaled, 1)

            pairs(act, NCH, scale)

        @block.vector
        def _(dve):
            v = nc.vector
            v.memset(e_src_i[PAD0:P, :], 0)
            v.memset(e_dst_i[PAD0:P, :], NB * P - 1)
            v.memset(adx[:, MARGIN + (NB - 1) * D:COLS], 0.0)
            v.memset(adx[:, 0:MARGIN], 0.0)
            v.memset(msgb[:], 0.0)
            v.memset(flags[:], 0.0)
            v.memset(b_msg_all[:], 0.0)
            v.memset(ones[:], 1.0)
            v.memset(zeros[:], 0.0)
            v.memset(eps[:], LN_EPS).then_inc(pads_set, 1)
            dve.wait_ge(consts, 5)
            v.tensor_copy(rowbase[:], rowbase_i[:])
            v.tensor_copy(jbase[:], jbase_i[:])
            v.tensor_copy(blkbase[:], blkbase_i[:])
            v.tensor_copy(win[:], select[:, 0].bitcast(I32)).then_inc(setup_dve, 1)
            dve.wait_ge(setup_dve, 1)

            dve.wait_ge(edges_in, 16 * EDGE_DMAS)
            v.tensor_copy(e_src[0:NB, :], e_src_i[0:NB, :])
            v.tensor_scalar(e_dst[0:NB, :], e_dst_i[0:NB, :], rowbase[0:NB, 0:1], None, ALU.subtract
                            ).then_inc(setup_dve, 1)
            dve.wait_ge(setup_dve, 2)
            in_window = e_dst_i.bitcast(F32)[0:NB, :]
            v.tensor_tensor(in_window.rearrange("p (j e) -> p j e", e=P),
                            e_dst[0:NB, :].rearrange("p (j e) -> p j e", e=P),
                            jbase[0:NB, :].unsqueeze(2).to_broadcast([NB, TPB, P]), ALU.subtract
                            ).then_inc(setup_dve, 1)
            dve.wait_ge(setup_dve, 3)
            v.tensor_reduce(flags[0:NB, 0:1], in_window, AX.X, ALU.max)
            v.tensor_reduce(flags[0:NB, 1:2], in_window, AX.X, ALU.min).then_inc(setup_dve, 1)
            dve.wait_ge(setup_dve, 4)
            v.tensor_scalar(flags[0:NB, 2:3], flags[0:NB, 0:1], float(P - MARGIN - 1), None, ALU.is_gt)
            v.tensor_scalar(flags[0:NB, 3:4], flags[0:NB, 1:2], float(-MARGIN), None, ALU.is_lt
                            ).then_inc(setup_dve, 1)
            dve.wait_ge(setup_dve, 5)
            v.tensor_tensor(flags[0:NB, 4:5], flags[0:NB, 2:3], flags[0:NB, 3:4], ALU.add
                            ).then_inc(setup_dve, 1)
            dve.wait_ge(flag_sum, 1)
            v.tensor_scalar(flags[:, 5:6], ps_w[:, 0:1], 1.0, None, ALU.min).then_inc(setup_dve, 1)
            dve.wait_ge(setup_dve, 7)
            v.tensor_copy(bad_i[:], flags[0:1, 5:6])
            v.tensor_scalar(flags[:, 6:7], flags[:, 5:6], OFF, None, ALU.mult).then_inc(flag_ready, 1)
            dve.wait_ge(flag_ready, 1)
            bad = dve.value_load(bad_i[0:1, 0:1], min_val=0, max_val=1)

            for n in range(2 * TURNS):
                q = n % TURNS * 4
                m = min(4, TPB - q)
                got = ps[:, n % 2, :].rearrange("p (j s) -> p j s", s=P)[:, 0:m, 0:NB]
                dve.wait_ge(edges_turned, n + 1)
                if n < TURNS:
                    v.tensor_copy(srcT[:, 0:NB, q:q + m].rearrange("p s j -> p j s"), got
                                  ).then_inc(edges_kept, 1)
                else:
                    v.tensor_scalar(dstT[:, :, q:q + m].rearrange("p s j -> p j s"), got,
                                    flags[:, 6:7], None, ALU.subtract).then_inc(edges_kept, 1)
            dve.wait_ge(edges_kept, 2 * TURNS)
            v.tensor_copy(srcT[:, NB:NB + 2, :], srcT[:, 0:2, :])
            v.tensor_copy(idx[:, 0, :], srcT[:, 0, :]).then_inc(idx_ready, 1)
            v.tensor_copy(idx[:, 1, :], srcT[:, 1, :]).then_inc(idx_ready, 1)

            dve.wait_ge(weights_turned, 1)
            v.tensor_copy(w_gates[:, 0:4].rearrange("p g n -> p (g n)"), ps_t)
            v.tensor_copy(w_gates[:, 4:6].rearrange("p g n -> p (g n)"), ps_c[:, 0:2 * P])
            dve.wait_ge(biases_spread, 1)
            v.tensor_copy(b_all[:], ps_m[:, 0:D + 1])
            v.tensor_copy(b_msg_all[:, 0:D], ps_m[:, 0:D])
            v.tensor_scalar(att_d_all[:], ones[:], att_d[:, 0:1], None, ALU.mult)
            v.tensor_tensor(b_rz[:], b_cols[:, 0:2], b_cols[:, 3:5], ALU.add).then_inc(weights_ready, 1)

            def stats(c, par, first):
                last = isinstance(c, int) and c == NCH - 1
                dve.wait_ge(x_in[par], (c - par) * 8 + (32 if last and LB > 1 else 16))
                for b in range(LB):
                    ins = v.bn_stats(st[:, par, b, :], adx[:, bass.ds(c * (LB * D) + (MARGIN + b * D), D)])
                ins.then_inc(ln_stats, 1)
                dve.wait_ge(ln_stats, c * 3 + 1)
                v.tensor_tensor(ln[:, par, 0], st[:, par, :, 1], st[:, par, :, 4], ALU.add)
                v.tensor_tensor(ln[:, par, 1], st[:, par, :, 1], st[:, par, :, 4], ALU.subtract)
                v.tensor_tensor(ln[:, par, 2], st[:, par, :, 2], st[:, par, :, 5], ALU.add
                                ).then_inc(ln_stats, 1)
                dve.wait_ge(ln_stats, c * 3 + 2)
                v.tensor_tensor(ln[:, par, 7], ln[:, par, 1], ln[:, par, 1], ALU.mult
                                ).then_inc(ln_stats, 1)
                dve.wait_ge(ln_stats, c * 3 + 3)
                v.scalar_tensor_tensor(out=ln[:, par, 3], in0=ln[:, par, 7], scalar=D / 4.0,
                                       in1=ln[:, par, 2], op0=ALU.mult, op1=ALU.add).then_inc(ln_var, 1)

            def finish(c, par):
                dve.wait_ge(ln_std, c + 1)
                if not (isinstance(c, int) and c < 2):
                    dve.wait_ge(ln_done, c - 1)
                v.reciprocal(ln[:, par, 5], ln[:, par, 4]).then_inc(ln_rstd, 1)
                dve.wait_ge(ln_rstd, c + 1)
                v.scalar_tensor_tensor(out=ln[:, par, 6], in0=ln[:, par, 0], scalar=-0.5,
                                       in1=ln[:, par, 5], op0=ALU.mult, op1=ALU.mult).then_inc(ln_ready, 1)

            stats(0, 0, True)
            stats(1, 1, True)
            finish(0, 0)
            if NCH > 4:
                with dve.Fori(1, NCH // 2 - 1, 1) as turn:
                    stats(turn * 2, 0, False)
                    finish(turn * 2 - 1, 1)
                    stats(turn * 2 + 1, 1, False)
                    finish(turn * 2, 0)
            if NCH > 2:
                stats(NCH - 2, 0, False)
                finish(NCH - 3, 1)
                stats(NCH - 1, 1, False)
                finish(NCH - 2, 0)
            finish(NCH - 1, 1)

            for c in range(2):
                dve.wait_ge(h0_out[c], 16 * (NCH // 2))
            v.memset(agg[:], 0.0).then_inc(agg_zeroed, 1)
            dve.wait_ge(agg_zeroed, 1)

            def general(layer):
                base = layer * TILES
                with dve.If(bad):
                    with dve.Fori(0, NB, 1) as i:
                        for j in range(TPB):
                            n = i * TPB + (j + base)
                            v.tensor_copy(gen_src[:, 0:1], srcT[:, bass.ds(i, 1), j])
                            v.tensor_tensor(gen_dst[:, 0:1], dstT[:, bass.ds(i, 1), j],
                                            blkbase[:, bass.ds(i, 1)], ALU.add).then_inc(gen_idx, 1)
                            dve.wait_ge(gen_idx, n + 1).then_inc(own_waits, 1)
                            with dve.Fori(0, NB, 1) as k:
                                u = n * NB + (k + 1)
                                if layer == 0:
                                    v.tensor_scalar(select[:, 0, 0], win[:, MARGIN // STRIDE], gen_dst[:, 0:1],
                                                    None, ALU.is_equal).then_inc(gen_sel, 1)
                                else:
                                    dve.wait_ge(gen_sig, u - TILES * NB)
                                    v.scalar_tensor_tensor(
                                        out=select[:, 0, 0], in0=win[:, MARGIN // STRIDE],
                                        scalar=gen_dst[:, 0:1], in1=gate[:, 0], op0=ALU.is_equal,
                                        op1=ALU.mult).then_inc(gen_sel, 1)
                                dve.wait_ge(gen_sel, u)
                                v.tensor_scalar(gen_dst[:, 0:1], gen_dst[:, 0:1], float(P), None,
                                                ALU.subtract).then_inc(gen_next, 1)
                                dve.wait_ge(gen_mm, u)
                                v.tensor_tensor(agg[:, block_cols(k)], agg[:, block_cols(k)], ps_g, ALU.add
                                                ).then_inc(gen_add, 1)
                                dve.wait_ge(gen_next, u)
                                dve.wait_ge(gen_add, u)
                    dve.nop()

            def add_sums(layer, i, par, first):
                dve.wait_ge(sums_ready[layer], i + 1)
                if not (isinstance(i, int) and i == 0):
                    dve.wait_ge(sums_added[layer], i)
                to = agg[:, bass.ds(i * P, WIN)]
                v.tensor_tensor(to, to, ps_agg[:, par], ALU.add).then_inc(sums_added[layer], 1)

            def next_indices(i, par):
                v.tensor_copy(idx[:, par, :], srcT[:, bass.ds(i + 2, 1), :].rearrange("p s j -> p (s j)")
                              ).then_inc(idx_ready, 1)

            def nodes0(k, par):
                dve.wait_ge(n0_conv, k + 1)
                if not (isinstance(k, int) and k < 2):
                    dve.wait_ge(x1_out[par], (k - par) * 8)
                v.scalar_tensor_tensor(out=x1b[:, par], in0=ps_c[:, 0:D], scalar=0.0,
                                       in1=adx[:, block_cols(k)], op0=ALU.max, op1=ALU.add
                                       ).then_inc(n0_x1, 1)
                v.tensor_copy(agg[:, block_cols(k)], zeros[:])
                dve.wait_ge(n0_x1, k + 1)
                v.bn_stats(nst[:, par, 0:6], x1b[:, par]).then_inc(n0_stats, 1)
                dve.wait_ge(n0_stats, k + 1).then_inc(own_waits, 1)
                v.bn_aggr(nst[:, par, 6:8], nst[:, par, 0:6]).then_inc(n0_var, 1)
                dve.wait_ge(n0_std, k + 1)
                v.reciprocal(nst[:, par, 9:10], nst[:, par, 8:9]).then_inc(n0_rstd, 1)
                dve.wait_ge(n0_rstd, k + 1)
                v.tensor_scalar(hnb[:, par], x1b[:, par], nst[:, par, 6:7], nst[:, par, 9:10],
                                ALU.subtract, ALU.mult).then_inc(n0_norm, 1)
                dve.wait_ge(n0_proj, k + 1)
                if not (isinstance(k, int) and k < 2):
                    dve.wait_ge(msg_out[par], (k - par) * 8)
                v.tensor_tensor(msgb[:, par, 0:D + 1], ps_m[:, 0:D + 1], b_msg_all[:], ALU.add
                                ).then_inc(n0_msg, 1)

            def step0(i, par, first):
                v.tensor_tensor(select[:, par], dstT[:, bass.ds(i, 1), :].rearrange("p s j -> p (s j)")
                                .unsqueeze(2).to_broadcast([P, TPB, P]), win[:], ALU.is_equal
                                ).then_inc(sel_ready, 1)
                if not first:
                    nodes0(i - 2, par)
                add_sums(0, i, par, first)
                next_indices(i, par)

            general(0)
            pairs(dve, NB, step0)
            nodes0(NB - 2, 0)
            nodes0(NB - 1, 1)

            def mix1(k, par):
                dve.wait_ge(n1_rz, k + 1)
                v.scalar_tensor_tensor(out=tmp[:, 0], in0=ps_c[:, 2 * P:3 * P], scalar=b_cols[:, 5:6],
                                       in1=rz[:, 0], op0=ALU.add, op1=ALU.mult).then_inc(n1_rh, 1)
                dve.wait_ge(n1_rh, k + 1)
                v.tensor_tensor(tmp[:, 1], tmp[:, 0], ps_c[:, 3 * P:4 * P], ALU.add).then_inc(n1_pre, 1)

            def update1(k, par, width=P):
                dve.wait_ge(n1_cand, k + 1)
                v.tensor_tensor(tmp[:, 3], h1T[:, par], tmp[:, 2], ALU.subtract).then_inc(n1_diff, 1)
                dve.wait_ge(n1_diff, k + 1)
                v.tensor_tensor(tmp[:, 0], tmp[:, 3], rz[:, 1], ALU.mult).then_inc(n1_zd, 1)
                dve.wait_ge(n1_zd, k + 1)
                v.tensor_tensor(agg[:, block_cols(k)], tmp[:, 2], tmp[:, 0], ALU.add).then_inc(n1_hnew, 1)
                dve.wait_ge(n1_hnew, k + 1)
                v.bn_stats(bst[:, bass.ds(k, 1), :].rearrange("p s c -> p (s c)"),
                           agg[:, block_cols(k, width)]).then_inc(n1_bst, 1)

            def step1(i, par, first):
                for g, (j0, j1) in enumerate(GROUPS):
                    dve.wait_ge(gate_ready[g], i + 1)
                    for j in range(j0, j1):
                        last = v.scalar_tensor_tensor(out=select[:, par, j], in0=win[:, j],
                                                      scalar=dstT[:, bass.ds(i, 1), j], in1=gate[:, j],
                                                      op0=ALU.is_equal, op1=ALU.mult)
                    last.then_inc(att_ready[g], 1)
                    if not first and g == 1:
                        mix1(i - 2, par)
                    if not first and g == 2:
                        update1(i - 2, par)
                add_sums(1, i, par, first)
                if not (isinstance(i, int) and i >= NB - 2):
                    next_indices(i, par)

            general(1)
            pairs(dve, NB, step1, last_apart=True)
            for k in (NB - 2, NB - 1):
                mix1(k, k % 2)
                update1(k, k % 2, P if k < NB - 1 else TAIL)

            dve.wait_ge(n1_bst, NB)
            v.bn_aggr(bn[:, 0:2], bst[:].rearrange("p k c -> p (k c)")).then_inc(bn_dve, 1)
            dve.wait_ge(bn_std, 1)
            v.reciprocal(bn[:, 3:4], bn[:, 2:3]).then_inc(bn_dve, 1)
            dve.wait_ge(bn_dve, 2)
            v.tensor_tensor(bn[:, 4:5], bn[:, 3:4], b_cols[:, 6:7], ALU.mult).then_inc(bn_dve, 1)
            dve.wait_ge(bn_dve, 3)
            v.scalar_tensor_tensor(out=bn[:, 6:7], in0=bn[:, 0:1], scalar=bn[:, 4:5], in1=b_cols[:, 7:8],
                                   op0=ALU.mult, op1=ALU.subtract).then_inc(bn_dve, 1)
            dve.wait_ge(bn_dve, 4)
            v.tensor_scalar(bn[:, 5:6], bn[:, 6:7], -1.0, None, ALU.mult).then_inc(bn_dve, 1)

            for c in range(2):
                dve.wait_ge(x1_in[c], 16 * (NB // 2))

            def residual(c, par, first):
                dve.wait_ge(y_turned, c + 1)
                if not first:
                    dve.wait_ge(y_out[par], (c - par) * 8)
                v.tensor_tensor(out_s[:, par].rearrange("p b f -> p (b f)"), ps_y[par],
                                adx[:, bass.ds(c * (LB * D) + MARGIN, LB * D)], ALU.add).then_inc(y_added, 1)

            pairs(dve, NCH, residual)

        @block.tensor
        def _(pe):
            t = nc.tensor
            pe.wait_ge(setup_dve, 6)
            t.matmul(ps_w[:, 0:1], lhsT=ones[0:NB, :], rhs=flags[0:NB, 4:5], start=True, stop=True
                     ).then_inc(flag_sum, 1)
            for n in range(2 * TURNS):
                if n >= 2:
                    pe.wait_ge(edges_kept, n - 1)
                of = e_src if n < TURNS else e_dst
                for j in range(n % TURNS * 4, min(TPB, n % TURNS * 4 + 4)):
                    last = t.transpose(ps[:, n % 2, j % 4 * P:j % 4 * P + NB], of[0:NB, j * P:(j + 1) * P],
                                       ident[0:NB, 0:NB])
                last.then_inc(edges_turned, 1)
            pe.wait_ge(weights_in, 16 * 13)
            for g in range(6):
                to = ps_t[:, g * P:(g + 1) * P] if g < 4 else ps_c[:, (g - 4) * P:(g - 3) * P]
                last = t.transpose(to, w_in[:, g, :], ident[:])
            last.then_inc(weights_turned, 1)
            t.matmul(ps_m[:, 0:D + 1], lhsT=ones[0:1, :], rhs=b_row[:], start=True, stop=True
                     ).then_inc(biases_spread, 1)
            pe.wait_ge(flag_ready, 1)
            bad = pe.value_load(bad_i[0:1, 0:1], min_val=0, max_val=1)
            pe.wait_ge(weights_ready, 1)

            def general(layer):
                with pe.If(bad):
                    with pe.Fori(0, TILES, 1) as n:
                        pe.wait_ge(gen_gathered, n * 16 + 16 * (layer * TILES + 1)).then_inc(own_waits, 1)
                        with pe.Fori(0, NB, 1) as k:
                            pe.wait_ge(gen_sel, n * NB + (k + (layer * TILES * NB + 1)))
                            t.matmul(ps_g, lhsT=rows[:, 0, 0, 0:D], rhs=select[:, 0, 0], start=True, stop=True
                                     ).then_inc(gen_mm, 1)
                    pe.nop()

            def sums(layer, i, par, j):
                return t.matmul(ps_agg[:, par, STRIDE * j:STRIDE * j + P], lhsT=rows[:, par, j, 0:D],
                                rhs=select[:, par, j], start=(j == 0), stop=(j == TPB - 1),
                                skip_group_check=True)

            def free_sums(layer, i):
                if not (isinstance(i, int) and i < 2):
                    pe.wait_ge(sums_added[layer], i - 1)
                elif layer == 1:
                    pe.wait_ge(sums_added[0], NB)

            def turn_h0(k, par):
                pe.wait_ge(h0_in[par], (k - par) * 8 + 16)
                if not (isinstance(k, int) and k == 0):
                    pe.wait_ge(n0_h0T, k)
                t.transpose(ps_t[:, 0:P], h0b[:, par], ident[:]).then_inc(n0_turned, 1)

            def conv(k, par):
                pe.wait_ge(n0_agg, k + 1)
                if not (isinstance(k, int) and k == 0):
                    pe.wait_ge(n0_x1, k)
                t.matmul(ps_c[:, 0:D], lhsT=h0T[:, par], rhs=weight_s[:], start=True, stop=False)
                t.matmul(ps_c[:, 0:D], lhsT=aggs[:, par], rhs=weight_n[:], start=False, stop=True
                         ).then_inc(n0_conv, 1)

            def turn_norm(k, par):
                pe.wait_ge(n0_norm, k + 1)
                t.transpose(ps_h, hnb[:, par], ident[:]).then_inc(n0_hT, 1)

            def project(k, par):
                pe.wait_ge(n0_h1T, k + 1)
                if not (isinstance(k, int) and k == 0):
                    pe.wait_ge(n0_msg, k)
                    pe.wait_ge(n0_ad, k)
                t.matmul(ps_m[:, 0:D + 1], lhsT=h1T[:, par], rhs=weight_m[:], start=True, stop=True)
                t.matmul(ps_a, lhsT=att_d_all[:], rhs=h1T[:, par], start=True, stop=True
                         ).then_inc(n0_proj, 1)

            def step0(i, par, first):
                free_sums(0, i)
                pe.wait_ge(sel_ready, i + 1)
                for j in range(TPB):
                    pe.wait_ge(gathered[par * TPB + j], (i - par) * 8 + 16)
                    last = sums(0, i, par, j)
                    if not first and j == 1:
                        turn_h0(i - 2, par)
                    if not first and j == 4:
                        conv(i - 2, par)
                    if not first and j == 9:
                        turn_norm(i - 2, par)
                    if not first and j == 13:
                        project(i - 2, par)
                last.then_inc(sums_ready[0], 1)

            general(0)
            pairs(pe, NB, step0)
            for k in (NB - 2, NB - 1):
                turn_h0(k, k % 2)
                conv(k, k % 2)
                turn_norm(k, k % 2)
                project(k, k % 2)

            def gates(k, par):
                pe.wait_ge(sums_added[1], NB if isinstance(k, int) and k == NB - 1 else k + 2)
                pe.wait_ge(h1t_in[par], (k - par) * 8 + 16)
                if not (isinstance(k, int) and k == 0):
                    pe.wait_ge(n1_pre, k)
                block = agg[:, block_cols(k)]
                for g in range(2):
                    t.matmul(ps_c[:, g * P:(g + 1) * P], lhsT=w_gates[:, g], rhs=block, start=True, stop=False)
                    t.matmul(ps_c[:, g * P:(g + 1) * P], lhsT=w_gates[:, 3 + g], rhs=h1T[:, par],
                             start=False, stop=True)
                t.matmul(ps_c[:, 2 * P:3 * P], lhsT=w_gates[:, 5], rhs=h1T[:, par], start=True, stop=True)
                t.matmul(ps_c[:, 3 * P:4 * P], lhsT=w_gates[:, 2], rhs=block, start=True, stop=True
                         ).then_inc(n1_gates, 1)

            def step1(i, par, first):
                free_sums(1, i)
                for g, (j0, j1) in enumerate(GROUPS):
                    pe.wait_ge(att_ready[g], i + 1)
                    for j in range(j0, j1):
                        last = sums(1, i, par, j)
                    if not first and g == 0:
                        gates(i - 2, par)
                last.then_inc(sums_ready[1], 1)

            general(1)
            pairs(pe, NB, step1)
            gates(NB - 2, 0)
            gates(NB - 1, 1)

            def turn_y(c, par, first):
                pe.wait_ge(y_scaled, c + 1)
                if not first:
                    pe.wait_ge(y_added, c - 1)
                for b in range(LB):
                    last = t.transpose(ps_y[par][:, b * P:(b + 1) * P], y_s[:, par, b, :], ident[:])
                last.then_inc(y_turned, 1)

            pairs(pe, NCH, turn_y)


_INS = ["x", "src", "dst", "L0_gnn_w_s", "L0_gnn_w_n", "L1_gnn_W_msg", "L1_gnn_b_msg", "L1_gnn_W_att",
        "L1_gnn_b_att", "L1_gnn_W_ih", "L1_gnn_b_ih", "L1_gnn_W_hh", "L1_gnn_b_hh", "L1_gnn_gamma",
        "L1_gnn_beta"]


def kernel(**inputs):
    import numpy as np
    import concourse.bacc as bacc
    from concourse.bass_utils import run_bass_kernel_spmd

    nc = bacc.Bacc("TRN2", target_bir_lowering=False, num_devices=1)
    arrays, args = {}, []
    for name in _INS:
        a = np.ascontiguousarray(inputs[name])
        arrays[f"in_{name}"] = a
        args.append(nc.dram_tensor(f"in_{name}", a.shape, mybir.dt.from_np(a.dtype), kind="ExternalInput").ap())
    shape = arrays["in_x"].shape
    out = nc.dram_tensor("out_0", shape, F32, kind="ExternalOutput").ap()
    gnn_program(nc, *args, out)
    r = run_bass_kernel_spmd(nc, [arrays], core_ids=[0])
    return r.results[0]["out_0"]
```

```python
from contextlib import ExitStack

import concourse.bass as bass
from concourse import mybir

P = 128
D = 128
TPB = 17
STRIDE = 8
MARGIN = 64
ROW1 = 144
LN_EPS = 1e-5
BN_EPS = 1e-5
OFF = float(1 << 20)
GROUPS = ((0, 4), (4, 8), (8, 12), (12, TPB))
STEP_EDGES = TPB * P

ALU = mybir.AluOpType
ACT = mybir.ActivationFunctionType
AX = mybir.AxisListType
F32 = mybir.dt.float32
I32 = mybir.dt.int32


def pairs(eng, count, body, last_apart=False):
    turns = count // 2
    end = turns - 1 if last_apart and turns > 1 else turns
    body(0, 0, True)
    body(1, 1, True)
    if end > 1:
        with eng.Fori(1, end, 1) as turn:
            body(turn * 2, 0, False)
            body(turn * 2 + 1, 1, False)
    if end < turns:
        body(count - 2, 0, False)
        body(count - 1, 1, False)


def gnn_program(nc, x, src, dst, w_s, w_n, w_msg, b_msg, w_att, b_att, w_ih, b_ih, w_hh, b_hh,
                gamma, beta, out):
    N = x.shape[0]
    E = src.shape[0]
    NB = -(-N // P)
    assert NB % 2 == 0 and -(-E // STEP_EDGES) == NB and STRIDE * TPB >= P
    TAIL = N - (NB - 1) * P
    EFULL = E // STEP_EDGES
    ETAIL = E - EFULL * STEP_EDGES
    COLS = MARGIN + NB * P + MARGIN
    LB = 7 if NB % 14 == 0 else NB // 2
    NCH = NB // LB
    TILES = NB * TPB
    TURNS = -(-TPB // 4)
    WIN = STRIDE * (TPB - 1) + P
    PAD0 = EFULL // 32 * 32
    SLOTS = [(j0 + (j0 > 0), j1 + 1) for j0, j1 in GROUPS]
    EDGE_DMAS = ((PAD0 > 0) + EFULL - PAD0 + (ETAIL > 0))

    RAW = min(4 + NCH, NB)
    h0_table = nc.dram_tensor("h0_table", [NB * P, D], F32, kind="Internal").ap()
    msg_table = nc.dram_tensor("msg_table", [NB * P, ROW1], F32, kind="Internal").ap()
    x1_rows = nc.dram_tensor("x1_rows", [NB * P, D], F32, kind="Internal").ap()
    h1t_blocks = nc.dram_tensor("h1t_blocks", [NB, D, P], F32, kind="Internal").ap()

    ctx = ExitStack()
    with ctx:
        def sb(name, shape, dt=F32):
            return ctx.enter_context(nc.sbuf_tensor(name, shape, dt))

        def sem(name):
            return ctx.enter_context(nc.semaphore(name))

        agg = sb("agg", [P, COLS])
        adx = sb("adx", [P, COLS])
        srcT = sb("srcT", [P, NB + 2, TPB], I32)
        dstT = sb("dstT", [P, NB, TPB])
        idx = sb("idx", [P, 2, TPB], I32)
        rows = sb("rows", [P, 2, TPB, ROW1])
        win = sb("win", [P, TPB, P])
        select = sb("select", [P, 2, TPB, P])
        gate = sb("gate", [P, TPB, P])
        ident = sb("ident", [P, P])
        ones = sb("ones", [P, P])
        zeros = sb("zeros", [P, P])
        weight_s = sb("weight_s", [D, D])
        weight_n = sb("weight_n", [D, D])
        weight_m = sb("weight_m", [D, D + 1])
        att_d = sb("att_d", [D, 1])
        att_d_all = sb("att_d_all", [D, P])
        w_in = sb("w_in", [P, 6, D])
        w_gates = sb("w_gates", [D, 6, P])
        b_row = sb("b_row", [1, D + 1])
        b_all = sb("b_all", [P, D + 1])
        b_msg_all = sb("b_msg_all", [P, D + 1])
        b_cols = sb("b_cols", [P, 8])
        b_rz = sb("b_rz", [P, 2])
        eps = sb("eps", [P, 1])
        jbase = sb("jbase", [P, TPB])
        jbase_i = sb("jbase_i", [P, TPB], I32)
        rowbase = sb("rowbase", [P, 1])
        rowbase_i = sb("rowbase_i", [P, 1], I32)
        blkbase = sb("blkbase", [P, NB])
        blkbase_i = sb("blkbase_i", [P, NB], I32)
        flags = sb("flags", [P, 8])
        bad_i = sb("bad_i", [1, 1], I32)
        gen_dst = sb("gen_dst", [P, 1])
        gen_src = sb("gen_src", [P, 1], I32)
        gen_row = sb("gen_row", [P, ROW1])
        gen_ln = sb("gen_ln", [P, 12])
        row_stats = sb("row_stats", [P, TPB + 1, 6])
        row_mv = sb("row_mv", [P, TPB + 1, 2])
        row_std = sb("row_std", [P, TPB + 1])
        row_rstd = sb("row_rstd", [P, TPB + 1])
        row_shift = sb("row_shift", [P, TPB + 1])
        chunk_stats = sb("chunk_stats", [P, LB, 6])
        chunk_mv = sb("chunk_mv", [P, LB, 2])
        chunk_sc = sb("chunk_sc", [P, 3, LB])
        h0s = sb("h0s", [P, 2, LB, D])
        h0b = sb("h0b", [P, 2, D])
        h0T = sb("h0T", [D, 2, P])
        aggs = sb("aggs", [D, 2, P])
        x1b = sb("x1b", [P, 2, D])
        hnb = sb("hnb", [P, 2, D])
        h1T = sb("h1T", [D, 2, P])
        msgb = sb("msgb", [P, 2, ROW1])
        nst = sb("nst", [P, 2, 12])
        rz = sb("rz", [P, 2, 2, P])
        tmp = sb("tmp", [P, 2, 4, P])
        bst = sb("bst", [P, NB, 6])
        bn = sb("bn", [P, 8])

        STAGED = 4 * STEP_EDGES
        stage = agg if COLS >= STAGED else sb("stage", [P, STAGED])
        e_src_i = stage[:, 0:STEP_EDGES].bitcast(I32)
        e_dst_i = stage[:, STEP_EDGES:2 * STEP_EDGES].bitcast(I32)
        e_src = stage[:, 2 * STEP_EDGES:3 * STEP_EDGES]
        e_dst = stage[:, 3 * STEP_EDGES:4 * STEP_EDGES]
        y_s = select[:, :, 0:LB, :]
        out_s = rows[:, :, :, :].rearrange("p a t r -> p a (t r)")[:, :, 0:LB * D].rearrange(
            "p a (b f) -> p a b f", f=D)

        ps = ctx.enter_context(nc.psum_tensor("ps", [P, 8, 512], F32))
        ps_agg = ps[:, 0:2, 0:WIN]
        ps_t = ps[:, 2, :]
        ps_c = ps[:, 3, :]
        ps_m = ps[:, 4, :]
        ps_g = ps[:, 5, 0:P]
        ps_a = ps[:, 6, 0:P]
        ps_w = ps[:, 6, :]
        ps_h = ps[:, 7, 0:P]
        ps_g1 = [ps[:, 3 + c, :] for c in range(2)]
        ps_y = [ps[:, 2 * c:2 * c + 2, :].rearrange("p a b -> p (a b)")[:, 0:LB * D] for c in range(2)]

        def block_cols(k, w=P):
            return bass.ds(k * P + MARGIN, w)

        src_in = sem("src_in")
        dst_in = sem("dst_in")
        weights_in = sem("weights_in")
        x_in = sem("x_in")
        gathered = [sem(f"gathered{s}") for s in range(2 * TPB)]
        gen_gathered = sem("gen_gathered")
        x1_out = [sem(f"x1_out{c}") for c in range(2)]
        msg_out = [sem(f"msg_out{c}") for c in range(2)]
        h1t_out = [sem(f"h1t_out{c}") for c in range(2)]
        h1t_in = [sem(f"h1t_in{c}") for c in range(2)]
        x1_in = [sem(f"x1_in{c}") for c in range(2)]
        y_out = [sem(f"y_out{c}") for c in range(2)]
        pads_set = sem("pads_set")
        zero_set = sem("zero_set")
        consts = sem("consts")
        setup_dve = sem("setup_dve")
        flag_sum = sem("flag_sum")
        flag_ready = sem("flag_ready")
        edges_turned = sem("edges_turned")
        edges_kept = sem("edges_kept")
        weights_turned = sem("weights_turned")
        biases_spread = sem("biases_spread")
        weights_ready = sem("weights_ready")
        agg_zeroed = sem("agg_zeroed")
        stats_done = [sem(f"stats_done{g}") for g in range(len(GROUPS))]
        var_ready = [sem(f"var_ready{g}") for g in range(len(GROUPS))]
        std_ready = [sem(f"std_ready{g}") for g in range(len(GROUPS))]
        rstd_ready = [sem(f"rstd_ready{g}") for g in range(len(GROUPS))]
        shift_ready = [sem(f"shift_ready{g}") for g in range(len(GROUPS))]
        rows_normed = [sem(f"rows_normed{g}") for g in range(len(GROUPS))]
        chunk_stats_done = sem("chunk_stats_done")
        chunk_var = sem("chunk_var")
        chunk_std = sem("chunk_std")
        chunk_rstd = sem("chunk_rstd")
        chunk_shift = sem("chunk_shift")
        chunk_normed = sem("chunk_normed")
        h0_out = [sem(f"h0_out{c}") for c in range(2)]
        own_waits = sem("own_waits")
        gen_idx = sem("gen_idx")
        gen_ln_dve = sem("gen_ln_dve")
        gen_std = sem("gen_std")
        gen_normed = sem("gen_normed")
        gen_sig = sem("gen_sig")
        gen_sel = sem("gen_sel")
        gen_next = sem("gen_next")
        gen_mm = sem("gen_mm")
        gen_add = sem("gen_add")
        idx_ready = sem("idx_ready")
        sel_ready = sem("sel_ready")
        sums_ready = [sem(f"sums_ready{n}") for n in range(2)]
        sums_added = [sem(f"sums_added{n}") for n in range(2)]
        gate_ready = [sem(f"gate_ready{g}") for g in range(len(GROUPS))]
        att_ready = [sem(f"att_ready{g}") for g in range(len(GROUPS))]
        n0_turned = sem("n0_turned")
        n0_h0T = sem("n0_h0T")
        n0_agg = sem("n0_agg")
        n0_conv = sem("n0_conv")
        n0_x1 = sem("n0_x1")
        n0_stats = sem("n0_stats")
        n0_var = sem("n0_var")
        n0_std = sem("n0_std")
        n0_rstd = sem("n0_rstd")
        n0_norm = sem("n0_norm")
        n0_hT = sem("n0_hT")
        n0_h1T = sem("n0_h1T")
        n0_proj = sem("n0_proj")
        n0_msg = sem("n0_msg")
        n0_ad = sem("n0_ad")
        n1_gates = sem("n1_gates")
        n1_rz = sem("n1_rz")
        n1_rh = sem("n1_rh")
        n1_pre = sem("n1_pre")
        n1_cand = sem("n1_cand")
        n1_diff = sem("n1_diff")
        n1_zd = sem("n1_zd")
        n1_hnew = sem("n1_hnew")
        n1_bst = sem("n1_bst")
        bn_dve = sem("bn_dve")
        bn_std = sem("bn_std")
        y_scaled = sem("y_scaled")
        y_turned = sem("y_turned")
        y_added = sem("y_added")

        def adx_chunk(c, b):
            return adx[:, bass.ds(c * (LB * D) + (MARGIN + b * D), D)]

        def raw_and_table_steps(eng, raw_step, table_step):
            pairs(eng, NCH + 2, raw_step)
            for i in range(NCH + 2, RAW):
                raw_step(i, i % 2, False, False)
            if RAW < NB:
                with eng.Fori(RAW // 2, NB // 2, 1) as turn:
                    table_step(turn * 2, 0)
                    table_step(turn * 2 + 1, 1)

        block = ctx.enter_context(nc.Block())

        @block.sync
        def _(sp):
            for to, of, landed in ((e_src_i, src, src_in), (e_dst_i, dst, dst_in)):
                if PAD0:
                    sp.dma_start(to[0:PAD0, :], of[0:PAD0 * STEP_EDGES].rearrange(
                        "(p n) -> p n", n=STEP_EDGES)).then_inc(landed, 16)
                sp.wait_ge(pads_set, 1)
                for q in range(PAD0, EFULL + (ETAIL > 0)):
                    n = STEP_EDGES if q < EFULL else ETAIL
                    sp.dma_start(to[q:q + 1, 0:n], of[q * STEP_EDGES:q * STEP_EDGES + n].rearrange(
                        "(p n) -> p n", p=1)).then_inc(landed, 16)
            for c in range(NCH):
                full = LB if c < NCH - 1 else LB - 1
                if full:
                    sp.dma_start(
                        adx[:, MARGIN + c * LB * D:MARGIN + (c * LB + full) * D].rearrange(
                            "p (b f) -> p b f", f=D),
                        x[c * LB * P:(c * LB + full) * P, :].rearrange("(b p) f -> p b f", p=P),
                    ).then_inc(x_in, 16)
            sp.dma_start(adx[0:TAIL, MARGIN + (NB - 1) * D:MARGIN + NB * D],
                         x[(NB - 1) * P:N, :]).then_inc(x_in, 16)
            for to, of in ((weight_s[:], w_s), (weight_n[:], w_n), (weight_m[:, 0:D], w_msg),
                           (weight_m[:, D:D + 1], w_att[0:D, :]), (att_d[:], w_att[D:2 * D, :]),
                           (w_in[:, 0:3, :], w_ih.rearrange("(g p) d -> p g d", p=P)),
                           (w_in[:, 3:6, :], w_hh.rearrange("(g p) d -> p g d", p=P)),
                           (b_row[:, 0:D], b_msg.rearrange("(a d) -> a d", a=1)),
                           (b_row[:, D:D + 1], b_att.rearrange("(a d) -> a d", a=1)),
                           (b_cols[:, 0:3], b_ih.rearrange("(g p) -> p g", p=P)),
                           (b_cols[:, 3:6], b_hh.rearrange("(g p) -> p g", p=P)),
                           (b_cols[:, 6:7], gamma.rearrange("(p a) -> p a", a=1)),
                           (b_cols[:, 7:8], beta.rearrange("(p a) -> p a", a=1))):
                sp.dma_start(to, of, allow_slow_non_contiguous=True).then_inc(weights_in, 16)

            def nodes0(k, par, table=False):
                sp.wait_ge(n0_x1, k + 1)
                sp.dma_start(x1_rows[bass.ds(k * P, P), :], x1b[:, par]).then_inc(x1_out[par], 16)
                sp.wait_ge(n0_h1T, k + 1)
                sp.dma_start(h1t_blocks[bass.ds(k, 1)].rearrange("a f n -> f (a n)"),
                             h1T[:, par]).then_inc(h1t_out[par], 16)
                sp.wait_ge(n0_msg, k + 1)
                sp.dma_start(msg_table[bass.ds(k * P, P), :], msgb[:, par]).then_inc(msg_out[par], 16)
                if table:
                    sp.wait_ge(chunk_normed, k + 1)
                    sp.dma_start(h0_table[bass.ds(k * (LB * P), LB * P), :].rearrange(
                        "(b p) f -> p b f", p=P), h0s[:, par]).then_inc(h0_out[par], 16)

            with sp.Fori(0, NCH // 2, 1) as turn:
                nodes0(turn * 2, 0, True)
                nodes0(turn * 2 + 1, 1, True)
            with sp.Fori(NCH // 2, NB // 2, 1) as turn:
                nodes0(turn * 2, 0)
                nodes0(turn * 2 + 1, 1)
            for c in range(2):
                sp.wait_ge(x1_out[c], 16 * (NB // 2))
                sp.wait_ge(h1t_out[c], 16 * (NB // 2))

            def load_h1(k, par):
                sp.dma_start(h1T[:, par], h1t_blocks[bass.ds(k, 1)].rearrange("a f n -> f (a n)")
                             ).then_inc(h1t_in[par], 16)

            load_h1(0, 0)
            load_h1(1, 1)

            def nodes1(k, par, first):
                last = isinstance(k, int) and k >= NB - 2
                if not last:
                    sp.wait_ge(n1_diff, k + 1)
                    load_h1(k + 2, par)
                sp.wait_ge(att_ready[-1], NB if last else k + 2)
                sp.dma_start(adx[:, block_cols(k)], x1_rows[bass.ds(k * P, P), :]).then_inc(x1_in[par], 16)

            pairs(sp, NB, nodes1, last_apart=True)

            def store_y(c, par, first):
                sp.wait_ge(y_added, c + 1)
                last = isinstance(c, int) and c == NCH - 1
                full = LB - 1 if last else LB
                if full:
                    sp.dma_start(out[bass.ds(c * (LB * P), full * P), :].rearrange("(b p) f -> p b f", p=P),
                                 out_s[:, par, 0:full, :]).then_inc(y_out[par], 16)
                if last:
                    sp.dma_start(out[(NB - 1) * P:N, :], out_s[0:TAIL, par, LB - 1, :]
                                 ).then_inc(y_out[par], 16)

            pairs(sp, NCH, store_y, last_apart=True)
            sp.wait_ge(y_out[0], 16 * (NCH // 2))
            sp.wait_ge(y_out[1], 16 * (NCH // 2 + (1 if LB > 1 else 0)))

        @block.gpsimd
        def _(pool):
            nc.gpsimd.memset(ident[:], 0.0).then_inc(zero_set, 1)
            pool.wait_ge(zero_set, 1)
            nc.gpsimd.affine_select(out=ident[:], in_=ident[:], compare_op=ALU.not_equal, fill=1.0, base=0,
                                    pattern=[[-1, P]], channel_multiplier=1).then_inc(consts, 1)
            nc.gpsimd.iota(rowbase_i[:], pattern=[[0, 1]], base=0, channel_multiplier=P).then_inc(consts, 1)
            nc.gpsimd.iota(jbase_i[:], pattern=[[STRIDE, TPB]], base=0, channel_multiplier=0).then_inc(consts, 1)
            nc.gpsimd.iota(select[:, 0].bitcast(I32), pattern=[[STRIDE, TPB], [1, P]], base=-MARGIN,
                           channel_multiplier=0).then_inc(consts, 1)
            nc.gpsimd.iota(blkbase_i[:], pattern=[[P, NB]], base=1 << 20, channel_multiplier=0
                           ).then_inc(consts, 1)

            def gathers(layer, i, par, table, width):
                pool.wait_ge(idx_ready, i + (layer * NB + 1)).then_inc(own_waits, 1)
                for j in range(TPB):
                    pool.indirect_dma_start(
                        out=rows[:, par, j, 0:width], out_offset=None, in_=table,
                        in_offset=bass.IndirectOffsetOnAxis(ap=idx[:, par, j:j + 1], axis=0)
                    ).then_inc(gathered[par * TPB + j], 16)

            def general(layer, table, width):
                with pool.If(bad):
                    with pool.Fori(0, TILES, 1) as t:
                        pool.wait_ge(gen_idx, t + (layer * TILES + 1)).then_inc(own_waits, 1)
                        pool.indirect_dma_start(
                            out=gen_row[:, 0:width], out_offset=None, in_=table,
                            in_offset=bass.IndirectOffsetOnAxis(ap=gen_src[:, 0:1], axis=0)
                        ).then_inc(gen_gathered, 16)
                    pool.nop()

            gathers(0, 0, 0, x, D)
            gathers(0, 1, 1, x, D)
            pool.wait_ge(flag_ready, 1)
            bad = pool.value_load(bad_i[0:1, 0:1], min_val=0, max_val=1)
            general(0, x, D)
            with pool.Fori(1, RAW // 2, 1) as turn:
                gathers(0, turn * 2, 0, x, D)
                gathers(0, turn * 2 + 1, 1, x, D)
            if RAW < NB:
                for c in range(2):
                    pool.wait_ge(h0_out[c], 16 * (NCH // 2))
                with pool.Fori(RAW // 2, NB // 2, 1) as turn:
                    gathers(0, turn * 2, 0, h0_table, D)
                    gathers(0, turn * 2 + 1, 1, h0_table, D)
            for c in range(2):
                pool.wait_ge(msg_out[c], 16 * (NB // 2))
            general(1, msg_table, ROW1)
            with pool.Fori(0, NB // 2, 1) as turn:
                gathers(1, turn * 2, 0, msg_table, ROW1)
                gathers(1, turn * 2 + 1, 1, msg_table, ROW1)

        @block.scalar
        def _(act):
            act.wait_ge(flag_ready, 1)
            bad = act.value_load(bad_i[0:1, 0:1], min_val=0, max_val=1)
            act.wait_ge(weights_ready, 1)

            with act.If(bad):
                with act.Fori(0, TILES, 1) as n:
                    act.wait_ge(gen_ln_dve, n * 4 + 2)
                    nc.scalar.activation(gen_ln[:, 8:9], gen_ln[:, 7:8], ACT.Sqrt, bias=eps[:, 0:1]
                                         ).then_inc(gen_std, 1)
                    act.wait_ge(gen_ln_dve, n * 4 + 4)
                    nc.scalar.activation(gen_row[:, 0:D], gen_row[:, 0:D], ACT.Relu, bias=gen_ln[:, 10:11],
                                         scale=gen_ln[:, 9:10]).then_inc(gen_normed, 1)
                act.nop()

            def root(i, g, own_only=False):
                a, b = (0, 1) if own_only else SLOTS[g]
                act.wait_ge(var_ready[g], i + 1)
                nc.scalar.activation(row_std[:, a:b], row_mv[:, a:b, 1], ACT.Sqrt, bias=eps[:, 0:1]
                                     ).then_inc(std_ready[g], 1)

            def norm(i, par, g, own_only=False):
                act.wait_ge(shift_ready[g], i + 1)
                if g == 0:
                    last = nc.scalar.activation(h0b[:, par], adx[:, block_cols(i)], ACT.Relu,
                                                bias=row_shift[:, 0:1], scale=row_rstd[:, 0:1])
                if not own_only:
                    for j in range(*GROUPS[g]):
                        last = nc.scalar.activation(rows[:, par, j, 0:D], rows[:, par, j, 0:D], ACT.Relu,
                                                    bias=row_shift[:, j + 1:j + 2],
                                                    scale=row_rstd[:, j + 1:j + 2])
                last.then_inc(rows_normed[g], 1)

            def keep_h0(i, par):
                act.wait_ge(n0_turned, i + 1)
                nc.scalar.copy(h0T[:, par], ps_t[:, 0:P]).then_inc(n0_h0T, 1)

            def chunk_root(c):
                act.wait_ge(chunk_var, c + 1)
                nc.scalar.activation(chunk_sc[:, 0], chunk_mv[:, :, 1], ACT.Sqrt, bias=eps[:, 0:1]
                                     ).then_inc(chunk_std, 1)

            def chunk_norm(c, par):
                act.wait_ge(chunk_shift, c + 1)
                if not (isinstance(c, int) and c < 2):
                    act.wait_ge(h0_out[par], (c - par) * 8)
                for b in range(LB):
                    last = nc.scalar.activation(
                        h0s[:, par, b, :], adx_chunk(c, b), ACT.Relu,
                        bias=chunk_sc[:, 2, b:b + 1], scale=chunk_sc[:, 1, b:b + 1])
                last.then_inc(chunk_normed, 1)

            def keep_sums(k, par):
                act.wait_ge(sums_added[0], NB if isinstance(k, int) and k == NB - 1 else k + 2)
                nc.scalar.copy(aggs[:, par], agg[:, block_cols(k)]).then_inc(n0_agg, 1)

            def std0(k, par):
                act.wait_ge(n0_var, k + 1)
                nc.scalar.activation(nst[:, par, 8:9], nst[:, par, 7:8], ACT.Sqrt, bias=eps[:, 0:1]
                                     ).then_inc(n0_std, 1)

            def keep_h1(k, par):
                act.wait_ge(n0_hT, k + 1)
                if not (isinstance(k, int) and k < 2):
                    act.wait_ge(h1t_out[par], (k - par) * 8)
                nc.scalar.activation(h1T[:, par], ps_h, ACT.Relu).then_inc(n0_h1T, 1)

            def keep_ad(k, par):
                act.wait_ge(n0_proj, k + 1)
                nc.scalar.activation(adx[:, block_cols(k)], ps_a, ACT.Identity,
                                     bias=b_all[:, D:D + 1]).then_inc(n0_ad, 1)

            def raw_step(i, par, first, build=True):
                if not first:
                    keep_sums(i - 2, par)
                root(i, 0)
                root(i, 1)
                norm(i, par, 0)
                root(i, 2)
                norm(i, par, 1)
                if build and not first:
                    chunk_root(i - 2)
                root(i, 3)
                if not first:
                    std0(i - 2, par)
                norm(i, par, 2)
                if not first:
                    keep_h1(i - 2, par)
                norm(i, par, 3)
                if build and not first:
                    chunk_norm(i - 2, par)
                    act.wait_ge(chunk_normed, i - 1)
                if not first:
                    keep_ad(i - 2, par)
                keep_h0(i, par)

            def table_step(i, par):
                keep_sums(i - 2, par)
                root(i, 0, True)
                norm(i, par, 0, True)
                std0(i - 2, par)
                keep_h0(i, par)
                keep_h1(i - 2, par)
                keep_ad(i - 2, par)

            raw_and_table_steps(act, raw_step, table_step)
            for stage in (keep_sums, std0, keep_h1, keep_ad):
                stage(NB - 2, 0)
                stage(NB - 1, 1)
            act.wait_ge(n0_ad, NB)

            with act.If(bad):
                with act.Fori(0, TILES, 1) as t:
                    act.wait_ge(gen_gathered, t * 16 + 16 * (TILES + 1))
                    with act.Fori(0, NB, 1) as k:
                        act.wait_ge(gen_add, t * NB + (k + TILES * NB))
                        nc.scalar.activation(gate[:, 0], adx[:, block_cols(k)], ACT.Sigmoid,
                                             bias=gen_row[:, D:D + 1]).then_inc(gen_sig, 1)
                act.wait_ge(gen_add, 2 * TILES * NB)
                act.nop()

            def gates1(k, par):
                act.wait_ge(n1_gates, k + 1)
                nc.scalar.activation(rz[:, par, 0], ps_g1[par][:, 0:P], ACT.Sigmoid, bias=b_rz[:, 0:1])
                nc.scalar.activation(rz[:, par, 1], ps_g1[par][:, P:2 * P], ACT.Sigmoid, bias=b_rz[:, 1:2]
                                     ).then_inc(n1_rz, 1)

            def cand1(k, par):
                act.wait_ge(n1_pre, k + 1)
                nc.scalar.activation(tmp[:, par, 2], tmp[:, par, 1], ACT.Tanh, bias=b_cols[:, 2:3]
                                     ).then_inc(n1_cand, 1)

            def step1(i, par, first):
                for g, (j0, j1) in enumerate(GROUPS):
                    if g == 0 and not (isinstance(i, int) and i == 0):
                        act.wait_ge(att_ready[-1], i)
                    for j in range(j0, j1):
                        act.wait_ge(gathered[par * TPB + j], (i - par) * 8 + 16 * (NB // 2 + 1))
                        last = nc.scalar.activation(
                            gate[:, j], adx[:, bass.ds(i * P + STRIDE * j, P)], ACT.Sigmoid,
                            bias=rows[:, par, j, D:D + 1])
                    last.then_inc(gate_ready[g], 1)
                    if not first and g == 1:
                        gates1(i - 2, par)
                    if not first and g == 2:
                        cand1(i - 2, par)

            pairs(act, NB, step1)
            for stage in (gates1, cand1):
                stage(NB - 2, 0)
                stage(NB - 1, 1)

            act.wait_ge(bn_dve, 1)
            nc.scalar.activation(bn[:, 2:3], bn[:, 1:2], ACT.Sqrt, bias=eps[:, 0:1]).then_inc(bn_std, 1)
            act.wait_ge(bn_dve, 5)

            def scale(c, par, first):
                if not first:
                    act.wait_ge(y_turned, c - 1)
                nc.scalar.activation(y_s[:, par], agg[:, bass.ds(c * (LB * P) + MARGIN, LB * P)].rearrange(
                    "p (b n) -> p b n", n=P), ACT.Identity, bias=bn[:, 5:6], scale=bn[:, 4:5]
                ).then_inc(y_scaled, 1)

            pairs(act, NCH, scale)

        @block.vector
        def _(dve):
            v = nc.vector
            v.memset(e_src_i[PAD0:P, :], 0)
            v.memset(e_dst_i[PAD0:P, :], NB * P - 1)
            v.memset(adx[:, MARGIN + (NB - 1) * D:COLS], 0.0)
            v.memset(adx[:, 0:MARGIN], 0.0)
            v.memset(msgb[:], 0.0)
            v.memset(flags[:], 0.0)
            v.memset(b_msg_all[:], 0.0)
            v.memset(ones[:], 1.0)
            v.memset(zeros[:], 0.0)
            v.memset(eps[:], LN_EPS).then_inc(pads_set, 1)
            dve.wait_ge(consts, 5)
            v.tensor_copy(rowbase[:], rowbase_i[:])
            v.tensor_copy(jbase[:], jbase_i[:])
            v.tensor_copy(blkbase[:], blkbase_i[:])
            v.tensor_copy(win[:], select[:, 0].bitcast(I32)).then_inc(setup_dve, 1)
            dve.wait_ge(setup_dve, 1)

            dve.wait_ge(src_in, 16 * EDGE_DMAS)
            v.tensor_copy(e_src[0:NB, :], e_src_i[0:NB, :]).then_inc(setup_dve, 1)
            turned = [0]

            def turned_tiles():
                for q in range(0, TPB, 4):
                    n = turned[0]
                    turned[0] += 1
                    dve.wait_ge(edges_turned, n + 1)
                    yield q, min(4, TPB - q), ps[:, n % 2, :].rearrange("p (j s) -> p j s", s=P)

            for q, m, got in turned_tiles():
                v.tensor_copy(srcT[:, 0:NB, q:q + m].rearrange("p s j -> p j s"), got[:, 0:m, 0:NB]
                              ).then_inc(edges_kept, 1)
            dve.wait_ge(edges_kept, TURNS)
            v.tensor_copy(idx[:, 0, :], srcT[:, 0, :]).then_inc(idx_ready, 1)
            v.tensor_copy(idx[:, 1, :], srcT[:, 1, :]).then_inc(idx_ready, 1)
            v.tensor_copy(srcT[:, NB:NB + 2, :], srcT[:, 0:2, :])

            dve.wait_ge(dst_in, 16 * EDGE_DMAS)
            v.tensor_scalar(e_dst[0:NB, :], e_dst_i[0:NB, :], rowbase[0:NB, 0:1], None, ALU.subtract
                            ).then_inc(setup_dve, 1)
            dve.wait_ge(setup_dve, 3)
            in_window = e_dst_i.bitcast(F32)[0:NB, :]
            v.tensor_tensor(in_window.rearrange("p (j e) -> p j e", e=P),
                            e_dst[0:NB, :].rearrange("p (j e) -> p j e", e=P),
                            jbase[0:NB, :].unsqueeze(2).to_broadcast([NB, TPB, P]), ALU.subtract
                            ).then_inc(setup_dve, 1)
            dve.wait_ge(setup_dve, 4)
            v.tensor_reduce(flags[0:NB, 0:1], in_window, AX.X, ALU.max)
            v.tensor_reduce(flags[0:NB, 1:2], in_window, AX.X, ALU.min).then_inc(setup_dve, 1)
            dve.wait_ge(setup_dve, 5)
            v.tensor_scalar(flags[0:NB, 2:3], flags[0:NB, 0:1], float(P - MARGIN - 1), None, ALU.is_gt)
            v.tensor_scalar(flags[0:NB, 3:4], flags[0:NB, 1:2], float(-MARGIN), None, ALU.is_lt
                            ).then_inc(setup_dve, 1)
            dve.wait_ge(setup_dve, 6)
            v.tensor_tensor(flags[0:NB, 4:5], flags[0:NB, 2:3], flags[0:NB, 3:4], ALU.add
                            ).then_inc(setup_dve, 1)
            dve.wait_ge(flag_sum, 1)
            v.tensor_scalar(flags[:, 5:6], ps_w[:, 0:1], 1.0, None, ALU.min).then_inc(setup_dve, 1)
            dve.wait_ge(setup_dve, 8)
            v.tensor_copy(bad_i[:], flags[0:1, 5:6])
            v.tensor_scalar(flags[:, 6:7], flags[:, 5:6], OFF, None, ALU.mult).then_inc(flag_ready, 1)
            dve.wait_ge(flag_ready, 1)
            bad = dve.value_load(bad_i[0:1, 0:1], min_val=0, max_val=1)

            for q, m, got in turned_tiles():
                v.tensor_scalar(dstT[:, :, q:q + m].rearrange("p s j -> p j s"), got[:, 0:m, 0:NB],
                                flags[:, 6:7], None, ALU.subtract).then_inc(edges_kept, 1)
            dve.wait_ge(edges_kept, 2 * TURNS)

            dve.wait_ge(weights_turned, 1)
            v.tensor_copy(w_gates[:, 0:4].rearrange("p g n -> p (g n)"), ps_t)
            v.tensor_copy(w_gates[:, 4:6].rearrange("p g n -> p (g n)"), ps_c[:, 0:2 * P])
            dve.wait_ge(biases_spread, 1)
            v.tensor_copy(b_all[:], ps_m[:, 0:D + 1])
            v.tensor_copy(b_msg_all[:, 0:D], ps_m[:, 0:D])
            v.tensor_scalar(att_d_all[:], ones[:], att_d[:, 0:1], None, ALU.mult)
            v.tensor_tensor(b_rz[:], b_cols[:, 0:2], b_cols[:, 3:5], ALU.add).then_inc(weights_ready, 1)

            v.memset(agg[:], 0.0).then_inc(agg_zeroed, 1)
            dve.wait_ge(agg_zeroed, 1)

            def general(layer):
                base = layer * TILES
                with dve.If(bad):
                    with dve.Fori(0, NB, 1) as i:
                        for j in range(TPB):
                            n = i * TPB + (j + base)
                            v.tensor_copy(gen_src[:, 0:1], srcT[:, bass.ds(i, 1), j])
                            v.tensor_tensor(gen_dst[:, 0:1], dstT[:, bass.ds(i, 1), j],
                                            blkbase[:, bass.ds(i, 1)], ALU.add).then_inc(gen_idx, 1)
                            dve.wait_ge(gen_idx, n + 1).then_inc(own_waits, 1)
                            if layer == 0:
                                dve.wait_ge(gen_gathered, n * 16 + 16).then_inc(own_waits, 1)
                                v.bn_stats(gen_ln[:, 0:6], gen_row[:, 0:D]).then_inc(gen_ln_dve, 1)
                                dve.wait_ge(gen_ln_dve, n * 4 + 1).then_inc(own_waits, 1)
                                v.bn_aggr(gen_ln[:, 6:8], gen_ln[:, 0:6]).then_inc(gen_ln_dve, 1)
                                dve.wait_ge(gen_std, n + 1)
                                v.reciprocal(gen_ln[:, 9:10], gen_ln[:, 8:9]).then_inc(gen_ln_dve, 1)
                                dve.wait_ge(gen_ln_dve, n * 4 + 3)
                                v.scalar_tensor_tensor(out=gen_ln[:, 10:11], in0=gen_ln[:, 6:7], scalar=-1.0,
                                                       in1=gen_ln[:, 9:10], op0=ALU.mult, op1=ALU.mult
                                                       ).then_inc(gen_ln_dve, 1)
                            with dve.Fori(0, NB, 1) as k:
                                u = n * NB + (k + 1)
                                if layer == 0:
                                    v.tensor_scalar(select[:, 0, 0], win[:, MARGIN // STRIDE], gen_dst[:, 0:1],
                                                    None, ALU.is_equal).then_inc(gen_sel, 1)
                                else:
                                    dve.wait_ge(gen_sig, u - TILES * NB)
                                    v.scalar_tensor_tensor(
                                        out=select[:, 0, 0], in0=win[:, MARGIN // STRIDE],
                                        scalar=gen_dst[:, 0:1], in1=gate[:, 0], op0=ALU.is_equal,
                                        op1=ALU.mult).then_inc(gen_sel, 1)
                                dve.wait_ge(gen_sel, u)
                                v.tensor_scalar(gen_dst[:, 0:1], gen_dst[:, 0:1], float(P), None,
                                                ALU.subtract).then_inc(gen_next, 1)
                                dve.wait_ge(gen_mm, u)
                                v.tensor_tensor(agg[:, block_cols(k)], agg[:, block_cols(k)], ps_g, ALU.add
                                                ).then_inc(gen_add, 1)
                                dve.wait_ge(gen_next, u)
                                dve.wait_ge(gen_add, u)
                    dve.nop()

            def add_sums(layer, i, par, first):
                dve.wait_ge(sums_ready[layer], i + 1)
                if not (isinstance(i, int) and i == 0):
                    dve.wait_ge(sums_added[layer], i)
                to = agg[:, bass.ds(i * P, WIN)]
                v.tensor_tensor(to, to, ps_agg[:, par], ALU.add).then_inc(sums_added[layer], 1)

            def next_indices(i, par):
                v.tensor_copy(idx[:, par, :], srcT[:, bass.ds(i + 2, 1), :].rearrange("p s j -> p (s j)")
                              ).then_inc(idx_ready, 1)

            def stats(i, par, g, own_only=False):
                a, b = (0, 1) if own_only else SLOTS[g]
                if g == 0:
                    last = v.bn_stats(row_stats[:, 0, :], adx[:, block_cols(i)])
                if not own_only:
                    for j in range(*GROUPS[g]):
                        dve.wait_ge(gathered[par * TPB + j], (i - par) * 8 + 16)
                        last = v.bn_stats(row_stats[:, j + 1, :], rows[:, par, j, 0:D])
                last.then_inc(stats_done[g], 1)
                dve.wait_ge(stats_done[g], i + 1).then_inc(own_waits, 1)
                for slot in range(a, b):
                    last = v.bn_aggr(row_mv[:, slot, :], row_stats[:, slot, :])
                last.then_inc(var_ready[g], 1)

            def shifts(i, g, own_only=False):
                a, b = (0, 1) if own_only else SLOTS[g]
                dve.wait_ge(std_ready[g], i + 1)
                v.reciprocal(row_rstd[:, a:b], row_std[:, a:b]).then_inc(rstd_ready[g], 1)
                dve.wait_ge(rstd_ready[g], i + 1)
                v.scalar_tensor_tensor(out=row_shift[:, a:b], in0=row_mv[:, a:b, 0], scalar=-1.0,
                                       in1=row_rstd[:, a:b], op0=ALU.mult, op1=ALU.mult
                                       ).then_inc(shift_ready[g], 1)

            def chunk_stat(c):
                if not (isinstance(c, int) and c == 0):
                    dve.wait_ge(chunk_normed, c)
                for b in range(LB):
                    last = v.bn_stats(chunk_stats[:, b, :], adx_chunk(c, b))
                last.then_inc(chunk_stats_done, 1)
                dve.wait_ge(chunk_stats_done, c + 1).then_inc(own_waits, 1)
                for b in range(LB):
                    last = v.bn_aggr(chunk_mv[:, b, :], chunk_stats[:, b, :])
                last.then_inc(chunk_var, 1)

            def chunk_shifts(c):
                dve.wait_ge(chunk_std, c + 1)
                v.reciprocal(chunk_sc[:, 1], chunk_sc[:, 0]).then_inc(chunk_rstd, 1)
                dve.wait_ge(chunk_rstd, c + 1)
                v.scalar_tensor_tensor(out=chunk_sc[:, 2], in0=chunk_mv[:, :, 0], scalar=-1.0,
                                       in1=chunk_sc[:, 1], op0=ALU.mult, op1=ALU.mult
                                       ).then_inc(chunk_shift, 1)

            def residual0(k, par):
                dve.wait_ge(n0_conv, k + 1)
                if not (isinstance(k, int) and k < 2):
                    dve.wait_ge(x1_out[par], (k - par) * 8)
                v.scalar_tensor_tensor(out=x1b[:, par], in0=ps_c[:, 0:D], scalar=0.0,
                                       in1=adx[:, block_cols(k)], op0=ALU.max, op1=ALU.add
                                       ).then_inc(n0_x1, 1)
                v.tensor_copy(agg[:, block_cols(k)], zeros[:])
                dve.wait_ge(n0_x1, k + 1)
                v.bn_stats(nst[:, par, 0:6], x1b[:, par]).then_inc(n0_stats, 1)
                dve.wait_ge(n0_stats, k + 1).then_inc(own_waits, 1)
                v.bn_aggr(nst[:, par, 6:8], nst[:, par, 0:6]).then_inc(n0_var, 1)

            def norm0(k, par):
                dve.wait_ge(n0_std, k + 1)
                v.reciprocal(nst[:, par, 9:10], nst[:, par, 8:9]).then_inc(n0_rstd, 1)
                dve.wait_ge(n0_rstd, k + 1)
                v.tensor_scalar(hnb[:, par], x1b[:, par], nst[:, par, 6:7], nst[:, par, 9:10],
                                ALU.subtract, ALU.mult).then_inc(n0_norm, 1)

            def message0(k, par):
                dve.wait_ge(n0_proj, k + 1)
                if not (isinstance(k, int) and k < 2):
                    dve.wait_ge(msg_out[par], (k - par) * 8)
                v.tensor_tensor(msgb[:, par, 0:D + 1], ps_m[:, 0:D + 1], b_msg_all[:], ALU.add
                                ).then_inc(n0_msg, 1)

            def select_windows(i, par):
                v.tensor_tensor(select[:, par], dstT[:, bass.ds(i, 1), :].rearrange("p s j -> p (s j)")
                                .unsqueeze(2).to_broadcast([P, TPB, P]), win[:], ALU.is_equal
                                ).then_inc(sel_ready, 1)

            def raw_step(i, par, first, build=True):
                stats(i, par, 0)
                select_windows(i, par)
                stats(i, par, 1)
                shifts(i, 0)
                if not first:
                    residual0(i - 2, par)
                stats(i, par, 2)
                shifts(i, 1)
                if build and not first:
                    chunk_stat(i - 2)
                stats(i, par, 3)
                if not first:
                    norm0(i - 2, par)
                shifts(i, 2)
                shifts(i, 3)
                if build and not first:
                    chunk_shifts(i - 2)
                if not first:
                    message0(i - 2, par)
                add_sums(0, i, par, first)
                next_indices(i, par)

            def table_step(i, par):
                stats(i, par, 0, True)
                select_windows(i, par)
                shifts(i, 0, True)
                residual0(i - 2, par)
                norm0(i - 2, par)
                message0(i - 2, par)
                add_sums(0, i, par, False)
                next_indices(i, par)

            dve.wait_ge(x_in, 16 * (NCH + (LB > 1)))
            general(0)
            raw_and_table_steps(dve, raw_step, table_step)
            for stage in (residual0, norm0, message0):
                stage(NB - 2, 0)
                stage(NB - 1, 1)

            def mix1(k, par):
                dve.wait_ge(n1_rz, k + 1)
                v.scalar_tensor_tensor(out=tmp[:, par, 0], in0=ps_g1[par][:, 2 * P:3 * P],
                                       scalar=b_cols[:, 5:6], in1=rz[:, par, 0], op0=ALU.add, op1=ALU.mult
                                       ).then_inc(n1_rh, 1)
                dve.wait_ge(n1_rh, k + 1)
                v.tensor_tensor(tmp[:, par, 1], tmp[:, par, 0], ps_g1[par][:, 3 * P:4 * P], ALU.add
                                ).then_inc(n1_pre, 1)

            def update1(k, par, width=P):
                dve.wait_ge(n1_cand, k + 1)
                v.tensor_tensor(tmp[:, par, 3], h1T[:, par], tmp[:, par, 2], ALU.subtract
                                ).then_inc(n1_diff, 1)
                dve.wait_ge(n1_diff, k + 1)
                v.tensor_tensor(tmp[:, par, 0], tmp[:, par, 3], rz[:, par, 1], ALU.mult).then_inc(n1_zd, 1)
                dve.wait_ge(n1_zd, k + 1)
                v.tensor_tensor(agg[:, block_cols(k)], tmp[:, par, 2], tmp[:, par, 0], ALU.add
                                ).then_inc(n1_hnew, 1)
                dve.wait_ge(n1_hnew, k + 1)
                v.bn_stats(bst[:, bass.ds(k, 1), :].rearrange("p s c -> p (s c)"),
                           agg[:, block_cols(k, width)]).then_inc(n1_bst, 1)

            def step1(i, par, first):
                for g, (j0, j1) in enumerate(GROUPS):
                    dve.wait_ge(gate_ready[g], i + 1)
                    for j in range(j0, j1):
                        last = v.scalar_tensor_tensor(out=select[:, par, j], in0=win[:, j],
                                                      scalar=dstT[:, bass.ds(i, 1), j], in1=gate[:, j],
                                                      op0=ALU.is_equal, op1=ALU.mult)
                    last.then_inc(att_ready[g], 1)
                    if not first and g == 1:
                        mix1(i - 2, par)
                    if not first and g == 2:
                        update1(i - 2, par)
                add_sums(1, i, par, first)
                if not (isinstance(i, int) and i >= NB - 2):
                    next_indices(i, par)

            general(1)
            pairs(dve, NB, step1, last_apart=True)
            mix1(NB - 2, 0)
            mix1(NB - 1, 1)
            update1(NB - 2, 0)
            update1(NB - 1, 1, TAIL)

            dve.wait_ge(n1_bst, NB)
            v.bn_aggr(bn[:, 0:2], bst[:].rearrange("p k c -> p (k c)")).then_inc(bn_dve, 1)
            dve.wait_ge(bn_std, 1)
            v.reciprocal(bn[:, 3:4], bn[:, 2:3]).then_inc(bn_dve, 1)
            dve.wait_ge(bn_dve, 2)
            v.tensor_tensor(bn[:, 4:5], bn[:, 3:4], b_cols[:, 6:7], ALU.mult).then_inc(bn_dve, 1)
            dve.wait_ge(bn_dve, 3)
            v.scalar_tensor_tensor(out=bn[:, 6:7], in0=bn[:, 0:1], scalar=bn[:, 4:5], in1=b_cols[:, 7:8],
                                   op0=ALU.mult, op1=ALU.subtract).then_inc(bn_dve, 1)
            dve.wait_ge(bn_dve, 4)
            v.tensor_scalar(bn[:, 5:6], bn[:, 6:7], -1.0, None, ALU.mult).then_inc(bn_dve, 1)

            for c in range(2):
                dve.wait_ge(x1_in[c], 16 * (NB // 2))

            def residual(c, par, first):
                dve.wait_ge(y_turned, c + 1)
                if not first:
                    dve.wait_ge(y_out[par], (c - par) * 8)
                v.tensor_tensor(out_s[:, par].rearrange("p b f -> p (b f)"), ps_y[par],
                                adx[:, bass.ds(c * (LB * D) + MARGIN, LB * D)], ALU.add).then_inc(y_added, 1)

            pairs(dve, NCH, residual)

        @block.tensor
        def _(pe):
            t = nc.tensor
            def turn_edges(of, n0):
                for n in range(n0, n0 + TURNS):
                    if n >= 2:
                        pe.wait_ge(edges_kept, n - 1)
                    for j in range((n - n0) * 4, min(TPB, (n - n0) * 4 + 4)):
                        last = t.transpose(ps[:, n % 2, j % 4 * P:j % 4 * P + NB],
                                           of[0:NB, j * P:(j + 1) * P], ident[0:NB, 0:NB])
                    last.then_inc(edges_turned, 1)

            pe.wait_ge(setup_dve, 2)
            turn_edges(e_src, 0)
            pe.wait_ge(setup_dve, 7)
            t.matmul(ps_w[:, 0:1], lhsT=ones[0:NB, :], rhs=flags[0:NB, 4:5], start=True, stop=True
                     ).then_inc(flag_sum, 1)
            turn_edges(e_dst, TURNS)
            pe.wait_ge(weights_in, 16 * 13)
            for g in range(6):
                to = ps_t[:, g * P:(g + 1) * P] if g < 4 else ps_c[:, (g - 4) * P:(g - 3) * P]
                last = t.transpose(to, w_in[:, g, :], ident[:])
            last.then_inc(weights_turned, 1)
            t.matmul(ps_m[:, 0:D + 1], lhsT=ones[0:1, :], rhs=b_row[:], start=True, stop=True
                     ).then_inc(biases_spread, 1)
            pe.wait_ge(flag_ready, 1)
            bad = pe.value_load(bad_i[0:1, 0:1], min_val=0, max_val=1)
            pe.wait_ge(weights_ready, 1)

            def general(layer):
                with pe.If(bad):
                    with pe.Fori(0, TILES, 1) as n:
                        if layer == 0:
                            pe.wait_ge(gen_normed, n + 1).then_inc(own_waits, 1)
                        else:
                            pe.wait_ge(gen_gathered, n * 16 + 16 * (TILES + 1)).then_inc(own_waits, 1)
                        with pe.Fori(0, NB, 1) as k:
                            pe.wait_ge(gen_sel, n * NB + (k + (layer * TILES * NB + 1)))
                            t.matmul(ps_g, lhsT=gen_row[:, 0:D], rhs=select[:, 0, 0], start=True, stop=True
                                     ).then_inc(gen_mm, 1)
                    pe.nop()

            def sums(layer, i, par, j):
                return t.matmul(ps_agg[:, par, STRIDE * j:STRIDE * j + P], lhsT=rows[:, par, j, 0:D],
                                rhs=select[:, par, j], start=(j == 0), stop=(j == TPB - 1),
                                skip_group_check=True)

            def free_sums(layer, i):
                if not (isinstance(i, int) and i < 2):
                    pe.wait_ge(sums_added[layer], i - 1)
                elif layer == 1:
                    pe.wait_ge(sums_added[0], NB)

            def turn_h0(k, par):
                pe.wait_ge(rows_normed[0], k + 1)
                if not (isinstance(k, int) and k == 0):
                    pe.wait_ge(n0_h0T, k)
                t.transpose(ps_t[:, 0:P], h0b[:, par], ident[:]).then_inc(n0_turned, 1)

            def conv(k, par):
                pe.wait_ge(n0_h0T, k + 1)
                pe.wait_ge(n0_agg, k + 1)
                if not (isinstance(k, int) and k == 0):
                    pe.wait_ge(n0_x1, k)
                t.matmul(ps_c[:, 0:D], lhsT=h0T[:, par], rhs=weight_s[:], start=True, stop=False)
                t.matmul(ps_c[:, 0:D], lhsT=aggs[:, par], rhs=weight_n[:], start=False, stop=True
                         ).then_inc(n0_conv, 1)

            def turn_norm(k, par):
                pe.wait_ge(n0_norm, k + 1)
                if not (isinstance(k, int) and k == 0):
                    pe.wait_ge(n0_h1T, k)
                t.transpose(ps_h, hnb[:, par], ident[:]).then_inc(n0_hT, 1)

            def project(k, par):
                pe.wait_ge(n0_h1T, k + 1)
                if not (isinstance(k, int) and k == 0):
                    pe.wait_ge(n0_msg, k)
                    pe.wait_ge(n0_ad, k)
                t.matmul(ps_m[:, 0:D + 1], lhsT=h1T[:, par], rhs=weight_m[:], start=True, stop=True)
                t.matmul(ps_a, lhsT=att_d_all[:], rhs=h1T[:, par], start=True, stop=True
                         ).then_inc(n0_proj, 1)

            def raw_step(i, par, first, build=True):
                free_sums(0, i)
                if not first:
                    conv(i - 2, par)
                pe.wait_ge(sel_ready, i + 1)
                for g, (j0, j1) in enumerate(GROUPS):
                    pe.wait_ge(rows_normed[g], i + 1)
                    for j in range(j0, j1):
                        last = sums(0, i, par, j)
                    if not first and g == 1:
                        turn_norm(i - 2, par)
                    if not first and g == 2:
                        project(i - 2, par)
                last.then_inc(sums_ready[0], 1)
                turn_h0(i, par)

            def table_step(i, par):
                free_sums(0, i)
                conv(i - 2, par)
                pe.wait_ge(sel_ready, i + 1)
                for j in range(TPB):
                    pe.wait_ge(gathered[par * TPB + j], (i - par) * 8 + 16)
                    last = sums(0, i, par, j)
                    if j == 2:
                        turn_h0(i, par)
                    if j == 7:
                        turn_norm(i - 2, par)
                    if j == 11:
                        project(i - 2, par)
                last.then_inc(sums_ready[0], 1)

            general(0)
            raw_and_table_steps(pe, raw_step, table_step)
            for stage in (conv, turn_norm, project):
                stage(NB - 2, 0)
                stage(NB - 1, 1)

            def gates(k, par):
                pe.wait_ge(sums_added[1], NB if isinstance(k, int) and k == NB - 1 else k + 2)
                pe.wait_ge(h1t_in[par], (k - par) * 8 + 16)
                block = agg[:, block_cols(k)]
                for g in range(2):
                    t.matmul(ps_g1[par][:, g * P:(g + 1) * P], lhsT=w_gates[:, g], rhs=block, start=True, stop=False)
                    t.matmul(ps_g1[par][:, g * P:(g + 1) * P], lhsT=w_gates[:, 3 + g], rhs=h1T[:, par],
                             start=False, stop=True)
                t.matmul(ps_g1[par][:, 2 * P:3 * P], lhsT=w_gates[:, 5], rhs=h1T[:, par], start=True, stop=True)
                t.matmul(ps_g1[par][:, 3 * P:4 * P], lhsT=w_gates[:, 2], rhs=block, start=True, stop=True
                         ).then_inc(n1_gates, 1)

            def step1(i, par, first):
                free_sums(1, i)
                for g, (j0, j1) in enumerate(GROUPS):
                    pe.wait_ge(att_ready[g], i + 1)
                    for j in range(j0, j1):
                        last = sums(1, i, par, j)
                    if not first and g == 0:
                        gates(i - 2, par)
                last.then_inc(sums_ready[1], 1)

            general(1)
            pairs(pe, NB, step1)
            gates(NB - 2, 0)
            gates(NB - 1, 1)

            def turn_y(c, par, first):
                pe.wait_ge(y_scaled, c + 1)
                if not first:
                    pe.wait_ge(y_added, c - 1)
                for b in range(LB):
                    last = t.transpose(ps_y[par][:, b * P:(b + 1) * P], y_s[:, par, b, :], ident[:])
                last.then_inc(y_turned, 1)

            pairs(pe, NCH, turn_y)


_INS = ["x", "src", "dst", "L0_gnn_w_s", "L0_gnn_w_n", "L1_gnn_W_msg", "L1_gnn_b_msg", "L1_gnn_W_att",
        "L1_gnn_b_att", "L1_gnn_W_ih", "L1_gnn_b_ih", "L1_gnn_W_hh", "L1_gnn_b_hh", "L1_gnn_gamma",
        "L1_gnn_beta"]


def kernel(**inputs):
    import numpy as np
    import concourse.bacc as bacc
    from concourse.bass_utils import run_bass_kernel_spmd

    nc = bacc.Bacc("TRN2", target_bir_lowering=False, num_devices=1)
    arrays, args = {}, []
    for name in _INS:
        a = np.ascontiguousarray(inputs[name])
        arrays[f"in_{name}"] = a
        args.append(nc.dram_tensor(f"in_{name}", a.shape, mybir.dt.from_np(a.dtype), kind="ExternalInput").ap())
    shape = arrays["in_x"].shape
    out = nc.dram_tensor("out_0", shape, F32, kind="ExternalOutput").ap()
    gnn_program(nc, *args, out)
    r = run_bass_kernel_spmd(nc, [arrays], core_ids=[0])
    return r.results[0]["out_0"]
```

```python
from contextlib import ExitStack

import concourse.bass as bass
from concourse import mybir

P = 128
D = 128
TPB = 17
STRIDE = 8
MARGIN = 64
TPC = 16
ROW1 = 144
LN_EPS = 1e-5
BN_EPS = 1e-5
OFF = float(1 << 20)
FAR = 4096.0
ROUND128 = 1.5 * 2.0 ** 30
GROUPS = ((0, 4), (4, 8), (8, 12), (12, TPB))
STEP_EDGES = TPB * P
GROUPS1 = ((0, 4), (4, 8), (8, 12), (12, TPC))
HALO = TPB + 2
REACH = [(TPB - 1, [0], TPC)] + [
    (j, [u for u in range(TPC) if -8 * j - 64 < (u - j + 1) * P and (u - j) * P < 192 - 8 * j], 0)
    for j in range(TPB)] + [(0, [TPC - 1], -TPC)]
PACKS = ((0, 7), (7, 13), (13, HALO))

ALU = mybir.AluOpType
ACT = mybir.ActivationFunctionType
AX = mybir.AxisListType
F32 = mybir.dt.float32
BF16 = mybir.dt.bfloat16
I32 = mybir.dt.int32


def pairs(eng, count, body, last_apart=False):
    turns = count // 2
    end = turns - 1 if last_apart and turns > 1 else turns
    body(0, 0, True)
    body(1, 1, True)
    if end > 1:
        with eng.Fori(1, end, 1) as turn:
            body(turn * 2, 0, False)
            body(turn * 2 + 1, 1, False)
    if end < turns:
        body(count - 2, 0, False)
        body(count - 1, 1, False)


def gnn_program(nc, x, src, dst, w_s, w_n, w_msg, b_msg, w_att, b_att, w_ih, b_ih, w_hh, b_hh,
                gamma, beta, out):
    N = x.shape[0]
    E = src.shape[0]
    NB = -(-N // P)
    assert NB % 2 == 0 and -(-E // STEP_EDGES) == NB and STRIDE * TPB >= P
    assert P * TPC == P * (TPB - 1) and STRIDE * TPC == P and E - N <= NB * TPC * P
    assert N < NB * P and N <= 1 << 15
    TAIL = N - (NB - 1) * P
    EFULL = E // STEP_EDGES
    ETAIL = E - EFULL * STEP_EDGES
    COLS = MARGIN + NB * P + MARGIN
    ZEROED = NB * 5 // 8 * P
    LB = 7 if NB % 14 == 0 else NB // 2
    NCH = NB // LB
    TILES = NB * TPB
    TURNS = -(-TPB // 4)
    WIN = STRIDE * (TPB - 1) + P
    WIN1 = STRIDE * (TPC - 1) + P
    PAD0 = EFULL // 32 * 32
    SLOTS = [(j0 + (j0 > 0), j1 + 1) for j0, j1 in GROUPS]
    assert ETAIL > 1
    LAST = [min(TPB, -(-ETAIL // (2 * P)) * 2),
            min(TPC, -(-(E - N - (NB - 1) * TPC * P) // (2 * P)) * 2)]
    assert E - N > (NB - 1) * TPC * P
    EDGE_DMAS = ((PAD0 > 0) + EFULL - PAD0 + (ETAIL > 0))

    RAW = 4 + NCH
    PARTS = 8
    assert RAW + PARTS < NB
    h0_table = nc.dram_tensor("h0_table", [NB * P, D], F32, kind="Internal").ap()
    msg_table = nc.dram_tensor("msg_table", [NB * P, ROW1], F32, kind="Internal").ap()
    x1_rows = nc.dram_tensor("x1_rows", [NB * P, D], F32, kind="Internal").ap()
    h1t_blocks = nc.dram_tensor("h1t_blocks", [NB, D, P], F32, kind="Internal").ap()

    ctx = ExitStack()
    with ctx:
        def sb(name, shape, dt=F32):
            return ctx.enter_context(nc.sbuf_tensor(name, shape, dt))

        def sem(name):
            return ctx.enter_context(nc.semaphore(name))

        agg = sb("agg", [P, COLS])
        adx = sb("adx", [P, COLS])
        srcT = sb("srcT", [P, NB + 2, TPB], I32)
        dstT = sb("dstT", [P, NB + 1, TPB])
        moveT = sb("moveT", [P, NB * TPB + 1], BF16)
        idx = sb("idx", [P, 2, TPB], I32)
        rows = sb("rows", [P, 2, TPB, ROW1])
        win = sb("win", [P, TPB, P])
        select = sb("select", [P, 2, TPB, P])
        gate = sb("gate", [P, TPB, P])
        ident = sb("ident", [P, P])
        ones = sb("ones", [P, P])
        zeros = sb("zeros", [P, P])
        weight_s = sb("weight_s", [D, D])
        weight_n = sb("weight_n", [D, D])
        weight_m = sb("weight_m", [D, D + 1])
        att_d = sb("att_d", [D, 1])
        att_d_all = sb("att_d_all", [D, P])
        w_in = sb("w_in", [P, 6, D])
        w_gates = sb("w_gates", [D, 6, P])
        b_row = sb("b_row", [1, D + 1])
        b_all = sb("b_all", [P, D + 1])
        b_msg_all = sb("b_msg_all", [P, D + 1])
        b_cols = sb("b_cols", [P, 9])
        b_rz = sb("b_rz", [P, 2])
        eps = sb("eps", [P, 1])
        jbase = sb("jbase", [P, TPB])
        jbase_i = sb("jbase_i", [P, TPB], I32)
        rowbase = sb("rowbase", [P, 1])
        rowbase_i = sb("rowbase_i", [P, 1], I32)
        blkbase = sb("blkbase", [P, NB])
        blkbase_i = sb("blkbase_i", [P, NB], I32)
        flags = sb("flags", [P, 8])
        flags1 = sb("flags1", [P, 20])
        limits = sb("limits", [P, 6])
        bad1_i = sb("bad1_i", [1, 1], I32)
        ebase = sb("ebase", [P, TPB])
        halo_shift = sb("halo_shift", [P, HALO])
        offsets = sb("offsets", [P, 4 * P], BF16)
        move_c = sb("move_c", [P, HALO])
        src_hi = sb("src_hi", [P, 2, HALO])
        values = sb("values", [P, HALO, 4], BF16)
        packed_s = sb("packed_s", [P, TPC, 4])
        packed_w = sb("packed_w", [P, 3, TPC])
        idxC = sb("idxC", [P, 2, TPC], I32)
        dstC = sb("dstC", [P, 2, TPC])
        att_all = sb("att_all", [D, P])
        self_sig = sb("self_sig", [P, P])
        self_msg = sb("self_msg", [P, P])
        bad_i = sb("bad_i", [1, 1], I32)
        gen_dst = sb("gen_dst", [P, 1])
        gen_src = sb("gen_src", [P, 1], I32)
        gen_row = sb("gen_row", [P, ROW1])
        gen_ln = sb("gen_ln", [P, 12])
        row_stats = sb("row_stats", [P, TPB + 1, 6])
        row_mv = sb("row_mv", [P, TPB + 1, 2])
        row_std = sb("row_std", [P, TPB + 1])
        row_rstd = sb("row_rstd", [P, TPB + 1])
        row_shift = sb("row_shift", [P, TPB + 1])
        chunk_stats = sb("chunk_stats", [P, LB, 6])
        chunk_mv = sb("chunk_mv", [P, LB, 2])
        chunk_sc = sb("chunk_sc", [P, 3, LB])
        h0s = sb("h0s", [P, 2, LB, D])
        h0b = sb("h0b", [P, 2, D])
        h0T = sb("h0T", [D, 2, P])
        aggs = sb("aggs", [D, 2, P])
        x1b = sb("x1b", [P, 2, D])
        hnb = sb("hnb", [P, 2, D])
        h1T = sb("h1T", [D, 2, P])
        msgb = sb("msgb", [P, 2, ROW1])
        nst = sb("nst", [P, 2, 12])
        rz = sb("rz", [P, 2, 2, P])
        tmp = sb("tmp", [P, 2, 4, P])
        bn = sb("bn", [P, 8])

        bst = (w_in.rearrange("p g d -> p (g d)")[:, 0:NB * 6].rearrange("p (k c) -> p k c", c=6)
               if NB <= P else sb("bst", [P, NB, 6]))

        STAGED = 4 * STEP_EDGES
        stage = agg if COLS >= STAGED else sb("stage", [P, STAGED])
        e_src_i = stage[:, 0:STEP_EDGES].bitcast(I32)
        e_dst_i = stage[:, STEP_EDGES:2 * STEP_EDGES].bitcast(I32)
        e_src = stage[:, 2 * STEP_EDGES:3 * STEP_EDGES]
        e_dst = stage[:, 3 * STEP_EDGES:4 * STEP_EDGES]
        next_i = gate.rearrange("p j e -> p (j e)").bitcast(I32)
        next_f = gate.rearrange("p j e -> p (j e)")
        work = next_f[:, 0:NB * TPB]
        work3 = work.rearrange("p (s j) -> p s j", j=TPB)
        moves = moveT[:, 0:NB * TPB]
        moves3 = moves.rearrange("p (s j) -> p s j", j=TPB)
        srcF = srcT.rearrange("p s j -> p (s j)")
        dstF = dstT.rearrange("p s j -> p (s j)")
        hot = h0s.rearrange("p a b f -> p (a b f)").bitcast(BF16)[:, 0:7 * 3 * P].rearrange(
            "p (s q) -> p s q", q=3 * P)
        assert 2 * LB <= TPB and NCH * LB == NB
        y_s = [select[:, c // 2, c % 2 * LB:(c % 2 + 1) * LB, :] for c in range(4)]
        out_s = [rows[:, c // 2].rearrange("p t r -> p (t r)")[:, c % 2 * LB * D:(c % 2 + 1) * LB * D
                                                              ].rearrange("p (b f) -> p b f", f=D)
                 for c in range(4)]

        ps = ctx.enter_context(nc.psum_tensor("ps", [P, 8, 512], F32))
        ps_agg = ps[:, 0:2, 0:WIN]
        ps_t = ps[:, 2, :]
        ps_c = ps[:, 3, :]
        ps_m = ps[:, 4, :]
        ps_g = ps[:, 5, 0:P]
        ps_n = ps[:, 5, :].rearrange("p (j s) -> p j s", s=P)
        ps_p = ps[:, 5, 0:4 * TPC]
        ps_a = ps[:, 6, 0:P]
        ps_w = ps[:, 6, :]
        ps_h = ps[:, 7, 0:P]
        ps_g1 = [ps[:, 3 + c, :] for c in range(2)]
        ps_y = [ps[:, 2 * c:2 * c + 2, :].rearrange("p a b -> p (a b)")[:, 0:LB * D] for c in range(4)]

        def block_cols(k, w=P):
            return bass.ds(k * P + MARGIN, w)

        src_in = sem("src_in")
        dst_in = sem("dst_in")
        weights_in = sem("weights_in")
        x_in = sem("x_in")
        PAIRS = -(-TPB // 2)
        gathered = [sem(f"gathered{s}") for s in range(2 * PAIRS)]
        gen_gathered = [sem(f"gen_gathered{n}") for n in range(2)]
        next_in = sem("next_in")
        x1_out = [sem(f"x1_out{c}") for c in range(2)]
        msg_out = [sem(f"msg_out{c}") for c in range(2)]
        h1t_out = [sem(f"h1t_out{c}") for c in range(2)]
        h1t_in = [sem(f"h1t_in{c}") for c in range(2)]
        x1_in = [sem(f"x1_in{c}") for c in range(2)]
        y_out = [sem(f"y_out{c}") for c in range(4)]
        pads_set = sem("pads_set")
        zero_set = sem("zero_set")
        consts = sem("consts")
        setup_dve = sem("setup_dve")
        flag_sum = sem("flag_sum")
        flag_ready = sem("flag_ready")
        edges_turned = sem("edges_turned")
        edges_kept = sem("edges_kept")
        weights_turned = sem("weights_turned")
        weights_ready = sem("weights_ready")
        agg_zeroed = sem("agg_zeroed")
        stats_done = [sem(f"stats_done{g}") for g in range(len(GROUPS))]
        var_ready = [sem(f"var_ready{g}") for g in range(len(GROUPS))]
        std_ready = [sem(f"std_ready{g}") for g in range(len(GROUPS))]
        rstd_ready = [sem(f"rstd_ready{g}") for g in range(len(GROUPS))]
        shift_ready = [sem(f"shift_ready{g}") for g in range(len(GROUPS))]
        rows_normed = [sem(f"rows_normed{g}") for g in range(len(GROUPS))]
        chunk_stats_done = sem("chunk_stats_done")
        chunk_var = sem("chunk_var")
        chunk_std = sem("chunk_std")
        chunk_rstd = sem("chunk_rstd")
        chunk_shift = sem("chunk_shift")
        chunk_normed = sem("chunk_normed")
        h0_out = [sem(f"h0_out{c}") for c in range(2)]
        own_waits = sem("own_waits")
        gen_idx = [sem(f"gen_idx{n}") for n in range(2)]
        gen_ln_dve = sem("gen_ln_dve")
        gen_std = sem("gen_std")
        gen_normed = sem("gen_normed")
        gen_sig = sem("gen_sig")
        gen_sel = [sem(f"gen_sel{n}") for n in range(2)]
        gen_next = [sem(f"gen_next{n}") for n in range(2)]
        gen_mm = [sem(f"gen_mm{n}") for n in range(2)]
        gen_add = [sem(f"gen_add{n}") for n in range(2)]
        next_pads = sem("next_pads")
        next_ready = sem("next_ready")
        next_turned = sem("next_turned")
        next_kept = sem("next_kept")
        prep = sem("prep")
        count1 = sem("count1")
        flag1_ready = sem("flag1_ready")
        values_parts = sem("values_parts")
        hot_ready = sem("hot_ready")
        packed = sem("packed")
        pack_kept = sem("pack_kept")
        pack_parts = sem("pack_parts")
        pack_ready = sem("pack_ready")
        self_proj = sem("self_proj")
        self_gate = sem("self_gate")
        self_prod = sem("self_prod")
        self_added = sem("self_added")
        idx_ready = sem("idx_ready")
        sel_ready = sem("sel_ready")
        sums_ready = [sem(f"sums_ready{n}") for n in range(2)]
        sums_added = [sem(f"sums_added{n}") for n in range(2)]
        gate_ready = [sem(f"gate_ready{g}") for g in range(len(GROUPS))]
        att_ready = [sem(f"att_ready{g}") for g in range(len(GROUPS))]
        n0_turned = sem("n0_turned")
        n0_h0T = sem("n0_h0T")
        n0_agg = sem("n0_agg")
        n0_conv = sem("n0_conv")
        n0_x1 = sem("n0_x1")
        n0_stats = sem("n0_stats")
        n0_var = sem("n0_var")
        n0_std = sem("n0_std")
        n0_rstd = sem("n0_rstd")
        n0_norm = sem("n0_norm")
        n0_hT = sem("n0_hT")
        n0_h1T = sem("n0_h1T")
        n0_proj = sem("n0_proj")
        n0_msg = sem("n0_msg")
        n0_ad = sem("n0_ad")
        n1_gates = sem("n1_gates")
        n1_rz = sem("n1_rz")
        n1_rh = sem("n1_rh")
        n1_pre = sem("n1_pre")
        n1_cand = sem("n1_cand")
        n1_diff = sem("n1_diff")
        n1_zd = sem("n1_zd")
        n1_hnew = sem("n1_hnew")
        n1_bst = sem("n1_bst")
        bn_dve = sem("bn_dve")
        bn_std = sem("bn_std")
        y_scaled = sem("y_scaled")
        y_turned = sem("y_turned")
        y_added = sem("y_added")

        def adx_chunk(c, b):
            return adx[:, bass.ds(c * (LB * D) + (MARGIN + b * D), D)]

        def raw_and_table_steps(eng, raw_step, table_step, parts):
            pairs(eng, NCH + 2, raw_step)
            for i in range(NCH + 2, RAW):
                raw_step(i, i % 2, False, False)
            for n, part in enumerate(parts):
                part()
                table_step(RAW + n, n % 2)
            if RAW + PARTS < NB - 2:
                with eng.Fori((RAW + PARTS) // 2, NB // 2 - 1, 1) as turn:
                    table_step(turn * 2, 0)
                    table_step(turn * 2 + 1, 1)
            table_step(NB - 2, 0)
            table_step(NB - 1, 1)

        block = ctx.enter_context(nc.Block())

        @block.sync
        def _(sp):
            for to, of, landed in ((e_src_i, src, src_in), (e_dst_i, dst, dst_in)):
                if PAD0:
                    sp.dma_start(to[0:PAD0, :], of[0:PAD0 * STEP_EDGES].rearrange(
                        "(p n) -> p n", n=STEP_EDGES)).then_inc(landed, 16)
                sp.wait_ge(pads_set, 1 if landed is src_in else 2)
                for q in range(PAD0, EFULL + (ETAIL > 0)):
                    n = STEP_EDGES if q < EFULL else ETAIL
                    sp.dma_start(to[q:q + 1, 0:n], of[q * STEP_EDGES:q * STEP_EDGES + n].rearrange(
                        "(p n) -> p n", p=1)).then_inc(landed, 16)
            sp.wait_ge(pads_set, 3)
            for c in range(NCH):
                full = LB if c < NCH - 1 else LB - 1
                if full:
                    sp.dma_start(
                        adx[:, MARGIN + c * LB * D:MARGIN + (c * LB + full) * D].rearrange(
                            "p (b f) -> p b f", f=D),
                        x[c * LB * P:(c * LB + full) * P, :].rearrange("(b p) f -> p b f", p=P),
                    ).then_inc(x_in, 16)
            sp.dma_start(adx[0:TAIL, MARGIN + (NB - 1) * D:MARGIN + NB * D],
                         x[(NB - 1) * P:N, :]).then_inc(x_in, 16)
            for to, of in ((weight_s[:], w_s), (weight_n[:], w_n), (weight_m[:, 0:D], w_msg),
                           (weight_m[:, D:D + 1], w_att[0:D, :]), (att_d[:], w_att[D:2 * D, :]),
                           (w_in[:, 0:3, :], w_ih.rearrange("(g p) d -> p g d", p=P)),
                           (w_in[:, 3:6, :], w_hh.rearrange("(g p) d -> p g d", p=P)),
                           (b_row[:, 0:D], b_msg.rearrange("(a d) -> a d", a=1)),
                           (b_row[:, D:D + 1], b_att.rearrange("(a d) -> a d", a=1)),
                           (b_cols[:, 0:3], b_ih.rearrange("(g p) -> p g", p=P)),
                           (b_cols[:, 3:6], b_hh.rearrange("(g p) -> p g", p=P)),
                           (b_cols[:, 8:9], b_msg.rearrange("(p a) -> p a", a=1)),
                           (b_cols[:, 6:7], gamma.rearrange("(p a) -> p a", a=1)),
                           (b_cols[:, 7:8], beta.rearrange("(p a) -> p a", a=1))):
                sp.dma_start(to, of, allow_slow_non_contiguous=True).then_inc(weights_in, 16)

            sp.wait_ge(next_pads, 1)
            if PAD0:
                sp.dma_start(next_i[0:PAD0, :], dst[1:1 + PAD0 * STEP_EDGES].rearrange(
                    "(p n) -> p n", n=STEP_EDGES)).then_inc(next_in, 16)
            for q in range(PAD0, EFULL + 1):
                n = STEP_EDGES if q < EFULL else ETAIL - 1
                sp.dma_start(next_i[q:q + 1, 0:n], dst[1 + q * STEP_EDGES:1 + q * STEP_EDGES + n].rearrange(
                    "(p n) -> p n", p=1)).then_inc(next_in, 16)

            def nodes0(k, par, table=False):
                sp.wait_ge(n0_x1, k + 1)
                sp.dma_start(x1_rows[bass.ds(k * P, P), :], x1b[:, par]).then_inc(x1_out[par], 16)
                sp.wait_ge(n0_h1T, k + 1)
                sp.dma_start(h1t_blocks[bass.ds(k, 1)].rearrange("a f n -> f (a n)"),
                             h1T[:, par]).then_inc(h1t_out[par], 16)
                sp.wait_ge(n0_msg, k + 1)
                sp.dma_start(msg_table[bass.ds(k * P, P), :], msgb[:, par]).then_inc(msg_out[par], 16)
                if table:
                    sp.wait_ge(chunk_normed, k + 1)
                    sp.dma_start(h0_table[bass.ds(k * (LB * P), LB * P), :].rearrange(
                        "(b p) f -> p b f", p=P), h0s[:, par]).then_inc(h0_out[par], 16)

            with sp.Fori(0, NCH // 2, 1) as turn:
                nodes0(turn * 2, 0, True)
                nodes0(turn * 2 + 1, 1, True)
            with sp.Fori(NCH // 2, NB // 2, 1) as turn:
                nodes0(turn * 2, 0)
                nodes0(turn * 2 + 1, 1)
            for c in range(2):
                sp.wait_ge(x1_out[c], 16 * (NB // 2))
                sp.wait_ge(h1t_out[c], 16 * (NB // 2))

            def load_h1(k, par):
                sp.dma_start(h1T[:, par], h1t_blocks[bass.ds(k, 1)].rearrange("a f n -> f (a n)")
                             ).then_inc(h1t_in[par], 16)

            load_h1(0, 0)
            load_h1(1, 1)

            def nodes1(k, par, first):
                last = isinstance(k, int) and k >= NB - 2
                if not last:
                    sp.wait_ge(n1_diff, k + 1)
                    load_h1(k + 2, par)
                sp.wait_ge(att_ready[-1], NB if last else k + 2)
                sp.dma_start(adx[:, block_cols(k)], x1_rows[bass.ds(k * P, P), :]).then_inc(x1_in[par], 16)

            pairs(sp, NB, nodes1, last_apart=True)

            for c in range(NCH):
                sp.wait_ge(y_added, c + 1)
                full = LB - 1 if c == NCH - 1 else LB
                if full:
                    sp.dma_start(out[c * LB * P:(c * LB + full) * P, :].rearrange("(b p) f -> p b f", p=P),
                                 out_s[c % 4][:, 0:full, :]).then_inc(y_out[c % 4], 16)
            sp.dma_start(out[(NB - 1) * P:N, :], out_s[(NCH - 1) % 4][0:TAIL, LB - 1, :]
                         ).then_inc(y_out[(NCH - 1) % 4], 16)
            for c in range(4):
                chunks = len(range(c, NCH, 4)) + (c == (NCH - 1) % 4 and LB > 1)
                sp.wait_ge(y_out[c], 16 * chunks)

        @block.gpsimd
        def _(pool):
            nc.gpsimd.memset(ident[:], 0.0).then_inc(zero_set, 1)
            pool.wait_ge(zero_set, 1)
            nc.gpsimd.affine_select(out=ident[:], in_=ident[:], compare_op=ALU.not_equal, fill=1.0, base=0,
                                    pattern=[[-1, P]], channel_multiplier=1).then_inc(consts, 1)
            nc.gpsimd.iota(rowbase_i[:], pattern=[[0, 1]], base=0, channel_multiplier=P).then_inc(consts, 1)
            nc.gpsimd.iota(jbase_i[:], pattern=[[STRIDE, TPB]], base=0, channel_multiplier=0).then_inc(consts, 1)
            nc.gpsimd.iota(select[:, 0].bitcast(I32), pattern=[[STRIDE, TPB], [1, P]], base=-MARGIN,
                           channel_multiplier=0).then_inc(consts, 1)
            nc.gpsimd.iota(blkbase_i[:], pattern=[[P, NB]], base=1 << 20, channel_multiplier=0
                           ).then_inc(consts, 1)

            def gathers(layer, i, par, table, width):
                pool.wait_ge(pack_ready if layer else idx_ready, i + 1).then_inc(own_waits, 1)
                of = idxC if layer else idx
                tiles = TPC if layer else TPB
                for j in range(LAST[layer] if isinstance(i, int) and i == NB - 1 else tiles):
                    pool.indirect_dma_start(
                        out=rows[:, par, j, 0:width], out_offset=None, in_=table,
                        in_offset=bass.IndirectOffsetOnAxis(ap=of[:, par, j:j + 1], axis=0)
                    ).then_inc(gathered[par * PAIRS + j // 2], 16)

            def general(layer, flag, table, width):
                with pool.If(flag):
                    with pool.Fori(0, TILES, 1) as t:
                        pool.wait_ge(gen_idx[layer], t + 1).then_inc(own_waits, 1)
                        pool.indirect_dma_start(
                            out=gen_row[:, 0:width], out_offset=None, in_=table,
                            in_offset=bass.IndirectOffsetOnAxis(ap=gen_src[:, 0:1], axis=0)
                        ).then_inc(gen_gathered[layer], 16)
                    pool.nop()

            gathers(0, 0, 0, x, D)
            gathers(0, 1, 1, x, D)
            nc.gpsimd.memset(next_i[PAD0:P, ETAIL - 1:], N).then_inc(next_pads, 1)
            pool.wait_ge(flag_ready, 1)
            bad = pool.value_load(bad_i[0:1, 0:1], min_val=0, max_val=1)
            general(0, bad, x, D)
            with pool.Fori(1, RAW // 2, 1) as turn:
                gathers(0, turn * 2, 0, x, D)
                gathers(0, turn * 2 + 1, 1, x, D)
            if RAW < NB:
                for c in range(2):
                    pool.wait_ge(h0_out[c], 16 * (NCH // 2))
                with pool.Fori(RAW // 2, NB // 2 - 1, 1) as turn:
                    gathers(0, turn * 2, 0, h0_table, D)
                    gathers(0, turn * 2 + 1, 1, h0_table, D)
                gathers(0, NB - 2, 0, h0_table, D)
                gathers(0, NB - 1, 1, h0_table, D)
            for c in range(2):
                pool.wait_ge(msg_out[c], 16 * (NB // 2))
            pool.wait_ge(flag1_ready, 1)
            bad1 = pool.value_load(bad1_i[0:1, 0:1], min_val=0, max_val=1)
            general(1, bad1, msg_table, ROW1)
            with pool.Fori(0, NB // 2 - 1, 1) as turn:
                gathers(1, turn * 2, 0, msg_table, ROW1)
                gathers(1, turn * 2 + 1, 1, msg_table, ROW1)
            gathers(1, NB - 2, 0, msg_table, ROW1)
            gathers(1, NB - 1, 1, msg_table, ROW1)

        @block.scalar
        def _(act):
            act.wait_ge(pads_set, 3)
            act.wait_ge(edges_turned, 2 * TURNS)
            nc.scalar.copy(agg[:, COLS - ZEROED:COLS].rearrange("p (b n) -> p b n", n=P),
                           zeros[:].unsqueeze(1).to_broadcast([P, ZEROED // P, P])).then_inc(agg_zeroed, 1)
            act.wait_ge(flag_ready, 1)
            bad = act.value_load(bad_i[0:1, 0:1], min_val=0, max_val=1)
            act.wait_ge(weights_ready, 1)

            with act.If(bad):
                with act.Fori(0, TILES, 1) as n:
                    act.wait_ge(gen_ln_dve, n * 4 + 2)
                    nc.scalar.activation(gen_ln[:, 8:9], gen_ln[:, 7:8], ACT.Sqrt, bias=eps[:, 0:1]
                                         ).then_inc(gen_std, 1)
                    act.wait_ge(gen_ln_dve, n * 4 + 4)
                    nc.scalar.activation(gen_row[:, 0:D], gen_row[:, 0:D], ACT.Relu, bias=gen_ln[:, 10:11],
                                         scale=gen_ln[:, 9:10]).then_inc(gen_normed, 1)
                act.nop()

            def root(i, g, own_only=False):
                a, b = (0, 1) if own_only else SLOTS[g]
                act.wait_ge(var_ready[g], i + 1)
                nc.scalar.activation(row_std[:, a:b], row_mv[:, a:b, 1], ACT.Sqrt, bias=eps[:, 0:1]
                                     ).then_inc(std_ready[g], 1)

            def norm(i, par, g, own_only=False):
                act.wait_ge(shift_ready[g], i + 1)
                if g == 0:
                    last = nc.scalar.activation(h0b[:, par], adx[:, block_cols(i)], ACT.Relu,
                                                bias=row_shift[:, 0:1], scale=row_rstd[:, 0:1])
                if not own_only:
                    for j in range(*GROUPS[g]):
                        last = nc.scalar.activation(rows[:, par, j, 0:D], rows[:, par, j, 0:D], ACT.Relu,
                                                    bias=row_shift[:, j + 1:j + 2],
                                                    scale=row_rstd[:, j + 1:j + 2])
                last.then_inc(rows_normed[g], 1)

            def keep_h0(i, par):
                act.wait_ge(n0_turned, i + 1)
                nc.scalar.copy(h0T[:, par], ps_t[:, 0:P]).then_inc(n0_h0T, 1)

            def chunk_root(c):
                act.wait_ge(chunk_var, c + 1)
                nc.scalar.activation(chunk_sc[:, 0], chunk_mv[:, :, 1], ACT.Sqrt, bias=eps[:, 0:1]
                                     ).then_inc(chunk_std, 1)

            def chunk_norm(c, par):
                act.wait_ge(chunk_shift, c + 1)
                if not (isinstance(c, int) and c < 2):
                    act.wait_ge(h0_out[par], (c - par) * 8)
                for b in range(LB):
                    last = nc.scalar.activation(
                        h0s[:, par, b, :], adx_chunk(c, b), ACT.Relu,
                        bias=chunk_sc[:, 2, b:b + 1], scale=chunk_sc[:, 1, b:b + 1])
                last.then_inc(chunk_normed, 1)

            def keep_sums(k, par):
                act.wait_ge(sums_added[0], NB if isinstance(k, int) and k == NB - 1 else k + 2)
                nc.scalar.copy(aggs[:, par], agg[:, block_cols(k)]).then_inc(n0_agg, 1)

            def std0(k, par):
                act.wait_ge(n0_var, k + 1)
                nc.scalar.activation(nst[:, par, 8:9], nst[:, par, 7:8], ACT.Sqrt, bias=eps[:, 0:1]
                                     ).then_inc(n0_std, 1)

            def keep_h1(k, par):
                act.wait_ge(n0_hT, k + 1)
                if not (isinstance(k, int) and k < 2):
                    act.wait_ge(h1t_out[par], (k - par) * 8)
                nc.scalar.activation(h1T[:, par], ps_h, ACT.Relu).then_inc(n0_h1T, 1)

            def keep_ad(k, par):
                act.wait_ge(n0_proj, k + 1)
                nc.scalar.activation(adx[:, block_cols(k)], ps_a, ACT.Identity,
                                     bias=b_all[:, D:D + 1]).then_inc(n0_ad, 1)

            def raw_step(i, par, first, build=True):
                if not first:
                    keep_sums(i - 2, par)
                root(i, 0)
                root(i, 1)
                norm(i, par, 0)
                root(i, 2)
                norm(i, par, 1)
                root(i, 3)
                norm(i, par, 2)
                if not first:
                    std0(i - 2, par)
                norm(i, par, 3)
                if not first:
                    keep_h1(i - 2, par)
                keep_h0(i, par)
                if build and not first:
                    chunk_root(i - 2)
                    chunk_norm(i - 2, par)
                    act.wait_ge(chunk_normed, i - 1)
                if not first:
                    keep_ad(i - 2, par)

            def table_step(i, par):
                keep_sums(i - 2, par)
                root(i, 0, True)
                norm(i, par, 0, True)
                std0(i - 2, par)
                keep_h0(i, par)
                keep_h1(i - 2, par)
                keep_ad(i - 2, par)

            raw_and_table_steps(act, raw_step, table_step, [lambda: None] * PARTS)
            for stage in (keep_sums, std0, keep_h1, keep_ad):
                stage(NB - 2, 0)
                stage(NB - 1, 1)
            act.wait_ge(n0_ad, NB)

            act.wait_ge(flag1_ready, 1)
            bad1 = act.value_load(bad1_i[0:1, 0:1], min_val=0, max_val=1)
            with act.If(bad1):
                with act.Fori(0, TILES, 1) as t:
                    act.wait_ge(gen_gathered[1], t * 16 + 16)
                    with act.Fori(0, NB, 1) as k:
                        act.wait_ge(gen_add[1], t * NB + (k + 1))
                        nc.scalar.activation(gate[:, 0], adx[:, block_cols(k)], ACT.Sigmoid,
                                             bias=gen_row[:, D:D + 1]).then_inc(gen_sig, 1)
                act.wait_ge(gen_add[1], TILES * NB + 1)
                act.nop()

            def gates1(k, par):
                act.wait_ge(n1_gates, k + 1)
                nc.scalar.activation(rz[:, par, 0], ps_g1[par][:, 0:P], ACT.Sigmoid, bias=b_rz[:, 0:1])
                nc.scalar.activation(rz[:, par, 1], ps_g1[par][:, P:2 * P], ACT.Sigmoid, bias=b_rz[:, 1:2]
                                     ).then_inc(n1_rz, 1)

            def cand1(k, par):
                act.wait_ge(n1_pre, k + 1)
                nc.scalar.activation(tmp[:, par, 2], tmp[:, par, 1], ACT.Tanh, bias=b_cols[:, 2:3]
                                     ).then_inc(n1_cand, 1)

            def self_gate1(k):
                act.wait_ge(self_proj, k + 1)
                if not (isinstance(k, int) and k == 0):
                    act.wait_ge(self_prod, k)
                nc.scalar.activation(self_sig[:], ps_t[:, P:2 * P], ACT.Sigmoid, bias=b_all[:, D:D + 1]
                                     ).then_inc(self_gate, 1)

            def step1(i, par, first):
                for g, (j0, j1) in enumerate(GROUPS1):
                    if not (isinstance(i, int) and i == 0):
                        act.wait_ge(att_ready[g], i)
                    for j in range(j0, j1):
                        if j % 2 == 0 and not (isinstance(i, int) and i == NB - 1 and j >= LAST[1]):
                            before = NB // 2 - (par == 1 and j >= LAST[0])
                            act.wait_ge(gathered[par * PAIRS + j // 2], (i - par) * 16 + 32 * (before + 1))
                        last = nc.scalar.activation(
                            gate[:, j], adx[:, bass.ds(i * P + STRIDE * j, P)], ACT.Sigmoid,
                            bias=rows[:, par, j, D:D + 1])
                    last.then_inc(gate_ready[g], 1)
                    if not first and g == 1:
                        gates1(i - 2, par)
                    if g == 2 and not (isinstance(i, int) and i == 0):
                        self_gate1(i - 1)
                    if not first and g == 3:
                        cand1(i - 2, par)

            pairs(act, NB, step1, last_apart=True)
            self_gate1(NB - 1)
            for stage in (gates1, cand1):
                stage(NB - 2, 0)
                stage(NB - 1, 1)

            act.wait_ge(bn_dve, 1)
            nc.scalar.activation(bn[:, 2:3], bn[:, 1:2], ACT.Sqrt, bias=eps[:, 0:1]).then_inc(bn_std, 1)
            act.wait_ge(bn_dve, 5)

            for c in range(NCH):
                if c >= 4:
                    act.wait_ge(y_turned, c - 3)
                nc.scalar.activation(y_s[c % 4], agg[:, MARGIN + c * LB * P:MARGIN + (c + 1) * LB * P].rearrange(
                    "p (b n) -> p b n", n=P), ACT.Identity, bias=bn[:, 5:6], scale=bn[:, 4:5]
                ).then_inc(y_scaled, 1)

        @block.vector
        def _(dve):
            v = nc.vector
            v.memset(e_src_i[PAD0:P, ETAIL:], N).then_inc(pads_set, 1)
            v.memset(e_dst_i[PAD0:P, ETAIL:], N).then_inc(pads_set, 1)
            v.memset(adx[:, MARGIN + (NB - 1) * D:COLS], 0.0)
            v.memset(adx[:, 0:MARGIN], 0.0)
            v.memset(msgb[:], 0.0)
            v.memset(flags[:], 0.0)
            v.memset(b_msg_all[:], 0.0)
            v.memset(ones[:], 1.0)
            v.memset(zeros[:], 0.0)
            v.memset(eps[:], LN_EPS).then_inc(pads_set, 1)
            dve.wait_ge(consts, 5)
            v.tensor_copy(rowbase[:], rowbase_i[:])
            v.tensor_copy(jbase[:], jbase_i[:])
            v.tensor_copy(blkbase[:], blkbase_i[:])
            v.tensor_copy(win[:], select[:, 0].bitcast(I32)).then_inc(setup_dve, 1)
            dve.wait_ge(setup_dve, 1)

            dve.wait_ge(src_in, 16 * EDGE_DMAS)
            v.tensor_copy(e_src[0:NB, :], e_src_i[0:NB, :]).then_inc(setup_dve, 1)
            turned = [0]

            def turned_tiles():
                for q in range(0, TPB, 4):
                    n = turned[0]
                    turned[0] += 1
                    dve.wait_ge(edges_turned, n + 1)
                    yield q, min(4, TPB - q), ps[:, n % 2, :].rearrange("p (j s) -> p j s", s=P)

            for q, m, got in turned_tiles():
                v.tensor_copy(srcT[:, 0:NB, q:q + m].rearrange("p s j -> p j s"), got[:, 0:m, 0:NB]
                              ).then_inc(edges_kept, 1)
            dve.wait_ge(edges_kept, TURNS)
            v.tensor_copy(idx[:, 0, :], srcT[:, 0, :]).then_inc(idx_ready, 1)
            v.tensor_copy(idx[:, 1, :], srcT[:, 1, :]).then_inc(idx_ready, 1)
            v.tensor_copy(srcT[:, NB:NB + 2, :], srcT[:, 0:2, :])

            dve.wait_ge(dst_in, 16 * EDGE_DMAS)
            v.tensor_scalar(e_dst[0:NB, :], e_dst_i[0:NB, :], rowbase[0:NB, 0:1], None, ALU.subtract
                            ).then_inc(setup_dve, 1)
            dve.wait_ge(setup_dve, 3)
            in_window = e_dst_i.bitcast(F32)[0:NB, :]
            v.tensor_tensor(in_window.rearrange("p (j e) -> p j e", e=P),
                            e_dst[0:NB, :].rearrange("p (j e) -> p j e", e=P),
                            jbase[0:NB, :].unsqueeze(2).to_broadcast([NB, TPB, P]), ALU.subtract
                            ).then_inc(setup_dve, 1)
            dve.wait_ge(setup_dve, 4)
            v.tensor_reduce(flags[0:NB, 0:1], in_window, AX.X, ALU.max)
            v.tensor_reduce(flags[0:NB, 1:2], in_window, AX.X, ALU.min).then_inc(setup_dve, 1)
            dve.wait_ge(setup_dve, 5)
            v.tensor_scalar(flags[0:NB, 2:3], flags[0:NB, 0:1], float(P - MARGIN - 1), None, ALU.is_gt)
            v.tensor_scalar(flags[0:NB, 3:4], flags[0:NB, 1:2], float(-MARGIN), None, ALU.is_lt
                            ).then_inc(setup_dve, 1)
            dve.wait_ge(setup_dve, 6)
            v.tensor_tensor(flags[0:NB, 4:5], flags[0:NB, 2:3], flags[0:NB, 3:4], ALU.add
                            ).then_inc(setup_dve, 1)
            dve.wait_ge(flag_sum, 1)
            v.tensor_scalar(flags[:, 5:6], ps_w[:, 0:1], 1.0, None, ALU.min).then_inc(setup_dve, 1)
            dve.wait_ge(setup_dve, 8)
            v.tensor_copy(bad_i[:], flags[0:1, 5:6])
            v.tensor_scalar(flags[:, 6:7], flags[:, 5:6], OFF, None, ALU.mult).then_inc(flag_ready, 1)
            dve.wait_ge(flag_ready, 1)
            bad = dve.value_load(bad_i[0:1, 0:1], min_val=0, max_val=1)

            for q, m, got in turned_tiles():
                v.tensor_scalar(dstT[:, 0:NB, q:q + m].rearrange("p s j -> p j s"), got[:, 0:m, 0:NB],
                                flags[:, 6:7], None, ALU.subtract).then_inc(edges_kept, 1)
            dve.wait_ge(edges_kept, 2 * TURNS)
            v.memset(dstT[:, NB, :], 0.0)
            v.memset(moveT[:, NB * TPB:NB * TPB + 1], FAR)

            dve.wait_ge(weights_turned, 1)
            v.tensor_copy(w_gates[:, 0:4].rearrange("p g n -> p (g n)"), ps_t)
            v.tensor_copy(w_gates[:, 4:6].rearrange("p g n -> p (g n)"), ps_c[:, 0:2 * P])
            dve.wait_ge(weights_turned, 2)
            v.tensor_copy(b_all[:], ps_m[:, 0:D + 1])
            v.tensor_copy(b_msg_all[:, 0:D], ps_m[:, 0:D])
            v.tensor_scalar(att_d_all[:], ones[:], att_d[:, 0:1], None, ALU.mult)
            v.tensor_tensor(b_rz[:], b_cols[:, 0:2], b_cols[:, 3:5], ALU.add).then_inc(weights_ready, 1)

            v.memset(agg[:, 0:COLS - ZEROED], 0.0).then_inc(agg_zeroed, 1)
            dve.wait_ge(agg_zeroed, 2)

            def general(layer, flag):
                with dve.If(flag):
                    if layer == 1:
                        v.tensor_scalar(dstF[:, 0:NB * TPB], dstF[:, 0:NB * TPB], flags1[:, 17:18], None,
                                        ALU.subtract).then_inc(gen_add[1], 1)
                        dve.wait_ge(gen_add[1], 1)
                    with dve.Fori(0, NB, 1) as i:
                        for j in range(TPB):
                            n = i * TPB + j
                            v.tensor_scalar(gen_src[:, 0:1], srcT[:, bass.ds(i, 1), j], float(N - 1), None,
                                            ALU.min)
                            v.tensor_tensor(gen_dst[:, 0:1], dstT[:, bass.ds(i, 1), j],
                                            blkbase[:, bass.ds(i, 1)], ALU.add).then_inc(gen_idx[layer], 1)
                            dve.wait_ge(gen_idx[layer], n + 1).then_inc(own_waits, 1)
                            if layer == 0:
                                dve.wait_ge(gen_gathered[0], n * 16 + 16).then_inc(own_waits, 1)
                                v.bn_stats(gen_ln[:, 0:6], gen_row[:, 0:D]).then_inc(gen_ln_dve, 1)
                                dve.wait_ge(gen_ln_dve, n * 4 + 1).then_inc(own_waits, 1)
                                v.bn_aggr(gen_ln[:, 6:8], gen_ln[:, 0:6]).then_inc(gen_ln_dve, 1)
                                dve.wait_ge(gen_std, n + 1)
                                v.reciprocal(gen_ln[:, 9:10], gen_ln[:, 8:9]).then_inc(gen_ln_dve, 1)
                                dve.wait_ge(gen_ln_dve, n * 4 + 3)
                                v.scalar_tensor_tensor(out=gen_ln[:, 10:11], in0=gen_ln[:, 6:7], scalar=-1.0,
                                                       in1=gen_ln[:, 9:10], op0=ALU.mult, op1=ALU.mult
                                                       ).then_inc(gen_ln_dve, 1)
                            with dve.Fori(0, NB, 1) as k:
                                u = n * NB + (k + 1)
                                if layer == 0:
                                    v.tensor_scalar(select[:, 0, 0], win[:, MARGIN // STRIDE], gen_dst[:, 0:1],
                                                    None, ALU.is_equal).then_inc(gen_sel[layer], 1)
                                else:
                                    dve.wait_ge(gen_sig, u)
                                    v.scalar_tensor_tensor(
                                        out=select[:, 0, 0], in0=win[:, MARGIN // STRIDE],
                                        scalar=gen_dst[:, 0:1], in1=gate[:, 0], op0=ALU.is_equal,
                                        op1=ALU.mult).then_inc(gen_sel[layer], 1)
                                dve.wait_ge(gen_sel[layer], u)
                                v.tensor_scalar(gen_dst[:, 0:1], gen_dst[:, 0:1], float(P), None,
                                                ALU.subtract).then_inc(gen_next[layer], 1)
                                dve.wait_ge(gen_mm[layer], u)
                                v.tensor_tensor(agg[:, block_cols(k)], agg[:, block_cols(k)], ps_g, ALU.add
                                                ).then_inc(gen_add[layer], 1)
                                dve.wait_ge(gen_next[layer], u)
                                dve.wait_ge(gen_add[layer], u + layer)
                    dve.nop()

            def add_sums(layer, i, par, first):
                dve.wait_ge(sums_ready[layer], i + 1)
                if not (isinstance(i, int) and i == 0):
                    dve.wait_ge(sums_added[layer], i)
                if layer == 1 and not (isinstance(i, int) and i == 0):
                    dve.wait_ge(self_added, i)
                width = WIN1 if layer else WIN
                to = agg[:, bass.ds(i * P, width)]
                v.tensor_tensor(to, to, ps_agg[:, par, 0:width], ALU.add).then_inc(sums_added[layer], 1)

            def next_indices(i, par):
                v.tensor_copy(idx[:, par, :], srcT[:, bass.ds(i + 2, 1), :].rearrange("p s j -> p (s j)")
                              ).then_inc(idx_ready, 1)

            def stats(i, par, g, own_only=False):
                a, b = (0, 1) if own_only else SLOTS[g]
                if g == 0:
                    last = v.bn_stats(row_stats[:, 0, :], adx[:, block_cols(i)])
                if not own_only:
                    for j in range(*GROUPS[g]):
                        if j % 2 == 0:
                            n = 8 if j == TPB - 1 else 16
                            dve.wait_ge(gathered[par * PAIRS + j // 2], (i - par) * n + 2 * n)
                        last = v.bn_stats(row_stats[:, j + 1, :], rows[:, par, j, 0:D])
                last.then_inc(stats_done[g], 1)
                dve.wait_ge(stats_done[g], i + 1).then_inc(own_waits, 1)
                for slot in range(a, b):
                    last = v.bn_aggr(row_mv[:, slot, :], row_stats[:, slot, :])
                last.then_inc(var_ready[g], 1)

            def shifts(i, g, own_only=False):
                a, b = (0, 1) if own_only else SLOTS[g]
                dve.wait_ge(std_ready[g], i + 1)
                v.reciprocal(row_rstd[:, a:b], row_std[:, a:b]).then_inc(rstd_ready[g], 1)
                dve.wait_ge(rstd_ready[g], i + 1)
                v.scalar_tensor_tensor(out=row_shift[:, a:b], in0=row_mv[:, a:b, 0], scalar=-1.0,
                                       in1=row_rstd[:, a:b], op0=ALU.mult, op1=ALU.mult
                                       ).then_inc(shift_ready[g], 1)

            def chunk_stat(c):
                if not (isinstance(c, int) and c == 0):
                    dve.wait_ge(chunk_normed, c)
                for b in range(LB):
                    last = v.bn_stats(chunk_stats[:, b, :], adx_chunk(c, b))
                last.then_inc(chunk_stats_done, 1)
                dve.wait_ge(chunk_stats_done, c + 1).then_inc(own_waits, 1)
                for b in range(LB):
                    last = v.bn_aggr(chunk_mv[:, b, :], chunk_stats[:, b, :])
                last.then_inc(chunk_var, 1)

            def chunk_shifts(c):
                dve.wait_ge(chunk_std, c + 1)
                v.reciprocal(chunk_sc[:, 1], chunk_sc[:, 0]).then_inc(chunk_rstd, 1)
                dve.wait_ge(chunk_rstd, c + 1)
                v.scalar_tensor_tensor(out=chunk_sc[:, 2], in0=chunk_mv[:, :, 0], scalar=-1.0,
                                       in1=chunk_sc[:, 1], op0=ALU.mult, op1=ALU.mult
                                       ).then_inc(chunk_shift, 1)

            def residual0(k, par):
                dve.wait_ge(n0_conv, k + 1)
                if not (isinstance(k, int) and k < 2):
                    dve.wait_ge(x1_out[par], (k - par) * 8)
                v.scalar_tensor_tensor(out=x1b[:, par], in0=ps_c[:, 0:D], scalar=0.0,
                                       in1=adx[:, block_cols(k)], op0=ALU.max, op1=ALU.add
                                       ).then_inc(n0_x1, 1)
                v.tensor_copy(agg[:, block_cols(k)], zeros[:])
                dve.wait_ge(n0_x1, k + 1)
                v.bn_stats(nst[:, par, 0:6], x1b[:, par]).then_inc(n0_stats, 1)
                dve.wait_ge(n0_stats, k + 1).then_inc(own_waits, 1)
                v.bn_aggr(nst[:, par, 6:8], nst[:, par, 0:6]).then_inc(n0_var, 1)

            def norm0(k, par):
                dve.wait_ge(n0_std, k + 1)
                v.reciprocal(nst[:, par, 9:10], nst[:, par, 8:9]).then_inc(n0_rstd, 1)
                dve.wait_ge(n0_rstd, k + 1)
                v.tensor_scalar(hnb[:, par], x1b[:, par], nst[:, par, 6:7], nst[:, par, 9:10],
                                ALU.subtract, ALU.mult).then_inc(n0_norm, 1)

            def message0(k, par):
                dve.wait_ge(n0_proj, k + 1)
                if not (isinstance(k, int) and k < 2):
                    dve.wait_ge(msg_out[par], (k - par) * 8)
                v.tensor_tensor(msgb[:, par, 0:D + 1], ps_m[:, 0:D + 1], b_msg_all[:], ALU.add
                                ).then_inc(n0_msg, 1)

            def select_windows(i, par):
                v.tensor_tensor(select[:, par], dstT[:, bass.ds(i, 1), :].rearrange("p s j -> p (s j)")
                                .unsqueeze(2).to_broadcast([P, TPB, P]), win[:], ALU.is_equal
                                ).then_inc(sel_ready, 1)

            def raw_step(i, par, first, build=True):
                stats(i, par, 0)
                select_windows(i, par)
                stats(i, par, 1)
                shifts(i, 0)
                if not first:
                    residual0(i - 2, par)
                stats(i, par, 2)
                shifts(i, 1)
                stats(i, par, 3)
                shifts(i, 2)
                shifts(i, 3)
                if not first:
                    norm0(i - 2, par)
                if build and not first:
                    chunk_stat(i - 2)
                add_sums(0, i, par, first)
                next_indices(i, par)
                if build and not first:
                    chunk_shifts(i - 2)
                if not first:
                    message0(i - 2, par)

            def table_step(i, par):
                stats(i, par, 0, True)
                select_windows(i, par)
                shifts(i, 0, True)
                residual0(i - 2, par)
                norm0(i - 2, par)
                message0(i - 2, par)
                add_sums(0, i, par, False)
                next_indices(i, par)

            dve.wait_ge(x_in, 16 * (NCH + (LB > 1)))
            def prepare_ends():
                dve.wait_ge(next_in, 16 * (EDGE_DMAS))
                v.tensor_scalar(next_f[0:NB, :], next_i[0:NB, :], rowbase[0:NB, 0:1], None, ALU.subtract
                                ).then_inc(next_ready, 1)
                for n in range(TURNS):
                    q, m = 4 * n, min(4, TPB - 4 * n)
                    dve.wait_ge(next_turned, n + 1)
                    v.tensor_tensor(moves3[:, :, q:q + m].rearrange("p s j -> p j s"), ps_n[:, 0:m, 0:NB],
                                    dstT[:, 0:NB, q:q + m].rearrange("p s j -> p j s"), ALU.subtract
                                    ).then_inc(next_kept, 1)

            def prepare_loops():
                dve.wait_ge(next_kept, TURNS)
                v.tensor_copy(work, srcF[:, 0:NB * TPB]).then_inc(prep, 1)
                dve.wait_ge(prep, 1)
                v.tensor_tensor(work, work, dstF[:, 0:NB * TPB], ALU.subtract).then_inc(prep, 1)
                dve.wait_ge(prep, 2)
                v.scalar_tensor_tensor(out=work3, in0=work3, scalar=OFF,
                                       in1=blkbase[:].unsqueeze(2).to_broadcast([P, NB, TPB]),
                                       op0=ALU.add, op1=ALU.subtract).then_inc(prep, 1)

            def prepare_check_loops():
                dve.wait_ge(prep, 3)
                v.tensor_tensor(work, work, moves, ALU.mult).then_inc(prep, 1)
                dve.wait_ge(prep, 4)
                v.tensor_reduce(flags1[:, 0:1], work, AX.X, ALU.max)
                v.tensor_reduce(flags1[:, 3:4], work, AX.X, ALU.min).then_inc(prep, 1)

            def prepare_check_ends():
                dve.wait_ge(prep, 5)
                v.tensor_copy(work, moves).then_inc(prep, 1)
                dve.wait_ge(prep, 6)
                v.tensor_reduce(flags1[:, 1:2], work, AX.X, ALU.max)
                v.tensor_reduce(flags1[:, 4:5], work, AX.X, ALU.min).then_inc(prep, 1)
                v.tensor_scalar(flags1[:, 19:20], rowbase[:], 1.0 / P, None, ALU.mult).then_inc(prep, 1)
                dve.wait_ge(prep, 8)

            def prepare_moves():
                v.tensor_scalar(work, dstF[:, 0:NB * TPB], flags1[:, 19:20], None, ALU.subtract).then_inc(prep, 1)
                v.tensor_scalar(ebase[:], jbase[:], float(P // STRIDE), flags1[:, 19:20], ALU.mult, ALU.add)
                v.tensor_tensor(flags1[:, 18:19], weight_m[:, D:D + 1], att_d[:], ALU.add)
                for k in range(4):
                    v.tensor_scalar(offsets[:, k * P:(k + 1) * P], win[:, MARGIN // STRIDE],
                                    float((k - 2) * P), None, ALU.add)
                v.memset(halo_shift[:], 0.0)
                v.memset(limits[:], 0.0)
                v.memset(values[:], 1.0)
                v.memset(flags1[:, 12:13], 0.0).then_inc(prep, 1)
                dve.wait_ge(prep, 10)
                v.memset(halo_shift[:, 0:1], -float(P))
                v.memset(halo_shift[:, HALO - 1:HALO], float(P))
                v.memset(limits[:, 1:2], 1.0)
                v.memset(limits[:, 2:3], float(TPC * (MARGIN - STRIDE)))
                v.memset(limits[:, 5:6], -float(TPC * MARGIN))
                v.tensor_scalar(att_all[:], ones[:], flags1[:, 18:19], None, ALU.mult)
                v.tensor_scalar(flags1[0:1, 12:13], dstT[0:1, 0, 0:1], 0.0, None, ALU.is_gt)
                v.scalar_tensor_tensor(out=moves, in0=moves, scalar=FAR, in1=work, op0=ALU.mult,
                                       op1=ALU.subtract).then_inc(prep, 1)
                dve.wait_ge(prep, 11)

            def prepare_flag():
                v.scalar_tensor_tensor(out=work3, in0=dstT[:, 0:NB, :], scalar=float(TPB),
                                       in1=ebase[:].unsqueeze(1).to_broadcast([P, NB, TPB]),
                                       op0=ALU.mult, op1=ALU.subtract).then_inc(prep, 1)
                dve.wait_ge(prep, 12)
                v.tensor_reduce(flags1[:, 2:3], work, AX.X, ALU.max)
                v.tensor_reduce(flags1[:, 5:6], work, AX.X, ALU.min).then_inc(prep, 1)
                dve.wait_ge(prep, 13)
                v.tensor_tensor(flags1[:, 6:9], flags1[:, 0:3], limits[:, 0:3], ALU.is_gt)
                v.tensor_tensor(flags1[:, 9:12], flags1[:, 3:6], limits[:, 3:6], ALU.is_lt).then_inc(prep, 1)
                dve.wait_ge(prep, 14)
                v.tensor_reduce(flags1[:, 13:14], flags1[:, 6:13], AX.X, ALU.add).then_inc(prep, 1)
                dve.wait_ge(count1, 1)
                v.tensor_tensor(flags1[:, 14:15], ps_p[:, 0:1], flags[:, 5:6], ALU.add).then_inc(prep, 1)
                dve.wait_ge(prep, 16)
                v.tensor_scalar(flags1[:, 14:15], flags1[:, 14:15], 1.0, None, ALU.min).then_inc(prep, 1)
                dve.wait_ge(prep, 17)
                v.tensor_scalar(flags1[:, 15:16], flags1[:, 14:15], -1.0, 1.0, ALU.mult, ALU.add)
                v.tensor_scalar(flags1[:, 16:17], flags1[:, 14:15], OFF, FAR, ALU.mult, ALU.add)
                v.tensor_scalar(flags1[:, 17:18], flags1[:, 14:15], OFF, flags[:, 6:7], ALU.mult, ALU.subtract)
                v.tensor_copy(bad1_i[:], flags1[0:1, 14:15]).then_inc(flag1_ready, 1)
                dve.wait_ge(flag1_ready, 1)

            def pack_values(c):
                a = 1 if isinstance(c, int) and c == 0 else 0
                of = bass.ds(c * TPB + (a - 1), HALO - a)
                v.tensor_copy(move_c[:, a:HALO], moveT[:, of])
                v.tensor_tensor(values[:, a:HALO, 2], dstF[:, of], halo_shift[:, a:HALO], ALU.add)
                v.tensor_scalar(src_hi[:, 0, a:HALO], srcF[:, of], ROUND128, None, ALU.add
                                ).then_inc(values_parts, 1)
                dve.wait_ge(values_parts, c * 3 + 1)
                v.tensor_scalar(src_hi[:, 1, a:HALO], src_hi[:, 0, a:HALO], ROUND128, None, ALU.subtract
                                ).then_inc(values_parts, 1)
                dve.wait_ge(values_parts, c * 3 + 2)
                v.tensor_copy(values[:, a:HALO, 0], src_hi[:, 1, a:HALO])
                v.tensor_tensor(values[:, a:HALO, 1], srcF[:, of], src_hi[:, 1, a:HALO], ALU.subtract
                                ).then_inc(values_parts, 1)
                dve.wait_ge(values_parts, c * 3 + 3)

            def pack_places(c, g):
                if not (isinstance(c, int) and c == 0 and g == 0):
                    dve.wait_ge(packed, c * 3 + g)
                for s in range(*PACKS[g]):
                    j, reach, frame = REACH[s]
                    if isinstance(c, int) and c == 0 and s == 0:
                        continue
                    k = reach[0] + frame - j + 2
                    w = len(reach) * P
                    last = v.tensor_scalar(hot[:, s - PACKS[g][0], 0:w], offsets[:, k * P:k * P + w],
                                           move_c[:, s:s + 1], None, ALU.is_equal)
                last.then_inc(hot_ready, 1)

            def pack_out(c, par):
                dve.wait_ge(packed, c * 3 + 3)
                v.tensor_copy(packed_s[:].rearrange("p u q -> p (u q)"), ps_p).then_inc(pack_kept, 1)
                dve.wait_ge(pack_kept, c + 1)
                v.tensor_tensor(packed_w[:, 0], packed_s[:, :, 0], packed_s[:, :, 1], ALU.add)
                v.scalar_tensor_tensor(out=packed_w[:, 1], in0=packed_s[:, :, 3], scalar=FAR,
                                       in1=packed_s[:, :, 2], op0=ALU.mult, op1=ALU.add
                                       ).then_inc(pack_parts, 1)
                dve.wait_ge(pack_parts, c * 2 + 1)
                v.tensor_scalar(packed_w[:, 2], packed_w[:, 0], flags1[:, 15:16], None, ALU.mult)
                v.tensor_scalar(dstC[:, par], packed_w[:, 1], flags1[:, 16:17], None, ALU.subtract
                                ).then_inc(pack_parts, 1)
                dve.wait_ge(pack_parts, c * 2 + 2)
                v.tensor_copy(idxC[:, par], packed_w[:, 2]).then_inc(pack_ready, 1)

            def pack_now(c):
                pack_values(c)
                for g in range(len(PACKS)):
                    pack_places(c, g)
                pack_out(c, c % 2)

            general(0, bad)
            raw_and_table_steps(dve, raw_step, table_step, [
                prepare_ends, prepare_loops, prepare_check_loops, prepare_check_ends, prepare_moves,
                prepare_flag, lambda: pack_now(0), lambda: pack_now(1)])
            for stage in (residual0, norm0, message0):
                stage(NB - 2, 0)
                stage(NB - 1, 1)

            def mix1(k, par):
                dve.wait_ge(n1_rz, k + 1)
                v.scalar_tensor_tensor(out=tmp[:, par, 0], in0=ps_g1[par][:, 2 * P:3 * P],
                                       scalar=b_cols[:, 5:6], in1=rz[:, par, 0], op0=ALU.add, op1=ALU.mult
                                       ).then_inc(n1_rh, 1)
                dve.wait_ge(n1_rh, k + 1)
                v.tensor_tensor(tmp[:, par, 1], tmp[:, par, 0], ps_g1[par][:, 3 * P:4 * P], ALU.add
                                ).then_inc(n1_pre, 1)

            def update1(k, par, width=P):
                dve.wait_ge(n1_cand, k + 1)
                v.tensor_tensor(tmp[:, par, 3], h1T[:, par], tmp[:, par, 2], ALU.subtract
                                ).then_inc(n1_diff, 1)
                dve.wait_ge(n1_diff, k + 1)
                v.tensor_tensor(tmp[:, par, 0], tmp[:, par, 3], rz[:, par, 1], ALU.mult).then_inc(n1_zd, 1)
                dve.wait_ge(n1_zd, k + 1)
                v.tensor_tensor(agg[:, block_cols(k)], tmp[:, par, 2], tmp[:, par, 0], ALU.add
                                ).then_inc(n1_hnew, 1)
                dve.wait_ge(n1_hnew, k + 1)
                v.bn_stats(bst[:, bass.ds(k, 1), :].rearrange("p s c -> p (s c)"),
                           agg[:, block_cols(k, width)]).then_inc(n1_bst, 1)

            def self_part1(k):
                dve.wait_ge(self_gate, k + 1)
                if not (isinstance(k, int) and k == 0):
                    dve.wait_ge(self_added, k)
                v.scalar_tensor_tensor(out=self_msg[:], in0=ps_t[:, 0:P], scalar=b_cols[:, 8:9],
                                       in1=self_sig[:], op0=ALU.add, op1=ALU.mult).then_inc(self_prod, 1)

            def self_add1(k):
                dve.wait_ge(self_prod, k + 1)
                dve.wait_ge(sums_added[1], k + 1)
                v.scalar_tensor_tensor(out=agg[:, block_cols(k)], in0=self_msg[:], scalar=flags1[:, 15:16],
                                       in1=agg[:, block_cols(k)], op0=ALU.mult, op1=ALU.add
                                       ).then_inc(self_added, 1)

            def step1(i, par, first):
                last_turn = isinstance(i, int) and i >= NB - 2
                if not last_turn:
                    pack_values(i + 2)
                for g, (j0, j1) in enumerate(GROUPS1):
                    dve.wait_ge(gate_ready[g], i + 1)
                    for j in range(j0, j1):
                        last = v.scalar_tensor_tensor(out=select[:, par, j], in0=win[:, j],
                                                      scalar=dstC[:, par, j:j + 1], in1=gate[:, j],
                                                      op0=ALU.is_equal, op1=ALU.mult)
                    last.then_inc(att_ready[g], 1)
                    if not first and g == 1:
                        mix1(i - 2, par)
                    if g < 3 and not last_turn:
                        pack_places(i + 2, g)
                if not (isinstance(i, int) and i == 0):
                    self_part1(i - 1)
                    self_add1(i - 1)
                if not first:
                    update1(i - 2, par)
                add_sums(1, i, par, first)
                if not last_turn:
                    pack_out(i + 2, par)

            bad1 = dve.value_load(bad1_i[0:1, 0:1], min_val=0, max_val=1)
            general(1, bad1)
            pairs(dve, NB, step1, last_apart=True)
            self_part1(NB - 1)
            self_add1(NB - 1)
            mix1(NB - 2, 0)
            mix1(NB - 1, 1)
            update1(NB - 2, 0)
            update1(NB - 1, 1, TAIL)

            dve.wait_ge(n1_bst, NB)
            v.bn_aggr(bn[:, 0:2], bst[:].rearrange("p k c -> p (k c)")).then_inc(bn_dve, 1)
            dve.wait_ge(bn_std, 1)
            v.reciprocal(bn[:, 3:4], bn[:, 2:3]).then_inc(bn_dve, 1)
            dve.wait_ge(bn_dve, 2)
            v.tensor_tensor(bn[:, 4:5], bn[:, 3:4], b_cols[:, 6:7], ALU.mult).then_inc(bn_dve, 1)
            dve.wait_ge(bn_dve, 3)
            v.scalar_tensor_tensor(out=bn[:, 6:7], in0=bn[:, 0:1], scalar=bn[:, 4:5], in1=b_cols[:, 7:8],
                                   op0=ALU.mult, op1=ALU.subtract).then_inc(bn_dve, 1)
            dve.wait_ge(bn_dve, 4)
            v.tensor_scalar(bn[:, 5:6], bn[:, 6:7], -1.0, None, ALU.mult).then_inc(bn_dve, 1)

            for c in range(2):
                dve.wait_ge(x1_in[c], 16 * (NB // 2))

            for c in range(NCH):
                dve.wait_ge(y_turned, c + 1)
                if c >= 4:
                    dve.wait_ge(y_out[c % 4], c // 4 * 16)
                v.tensor_tensor(out_s[c % 4].rearrange("p b f -> p (b f)"), ps_y[c % 4],
                                adx[:, MARGIN + c * LB * D:MARGIN + (c + 1) * LB * D], ALU.add
                                ).then_inc(y_added, 1)

        @block.tensor
        def _(pe):
            t = nc.tensor
            def turn_edges(of, n0):
                for n in range(n0, n0 + TURNS):
                    if n >= 2:
                        pe.wait_ge(edges_kept, n - 1)
                    for j in range((n - n0) * 4, min(TPB, (n - n0) * 4 + 4)):
                        last = t.transpose(ps[:, n % 2, j % 4 * P:j % 4 * P + NB],
                                           of[0:NB, j * P:(j + 1) * P], ident[0:NB, 0:NB])
                    last.then_inc(edges_turned, 1)

            pe.wait_ge(setup_dve, 2)
            turn_edges(e_src, 0)
            pe.wait_ge(setup_dve, 7)
            t.matmul(ps_w[:, 0:1], lhsT=ones[0:NB, :], rhs=flags[0:NB, 4:5], start=True, stop=True
                     ).then_inc(flag_sum, 1)
            turn_edges(e_dst, TURNS)
            pe.wait_ge(weights_in, 16 * 14)
            for g in range(6):
                to = ps_t[:, g * P:(g + 1) * P] if g < 4 else ps_c[:, (g - 4) * P:(g - 3) * P]
                last = t.transpose(to, w_in[:, g, :], ident[:])
            last.then_inc(weights_turned, 1)
            t.matmul(ps_m[:, 0:D + 1], lhsT=ones[0:1, :], rhs=b_row[:], start=True, stop=True
                     ).then_inc(weights_turned, 1)
            pe.wait_ge(flag_ready, 1)
            bad = pe.value_load(bad_i[0:1, 0:1], min_val=0, max_val=1)
            pe.wait_ge(weights_ready, 1)

            def general(layer, flag):
                with pe.If(flag):
                    with pe.Fori(0, TILES, 1) as n:
                        if layer == 0:
                            pe.wait_ge(gen_normed, n + 1).then_inc(own_waits, 1)
                        else:
                            pe.wait_ge(gen_gathered[1], n * 16 + 16).then_inc(own_waits, 1)
                        with pe.Fori(0, NB, 1) as k:
                            pe.wait_ge(gen_sel[layer], n * NB + (k + 1))
                            t.matmul(ps_g, lhsT=gen_row[:, 0:D], rhs=select[:, 0, 0], start=True, stop=True
                                     ).then_inc(gen_mm[layer], 1)
                    pe.nop()

            def sums(layer, i, par, j):
                return t.matmul(ps_agg[:, par, STRIDE * j:STRIDE * j + P], lhsT=rows[:, par, j, 0:D],
                                rhs=select[:, par, j], start=(j == 0), stop=(j == (TPC if layer else TPB) - 1),
                                skip_group_check=True)

            def free_sums(layer, i):
                if not (isinstance(i, int) and i < 2):
                    pe.wait_ge(sums_added[layer], i - 1)
                elif layer == 1:
                    pe.wait_ge(sums_added[0], NB)

            def turn_h0(k, par):
                pe.wait_ge(rows_normed[0], k + 1)
                if not (isinstance(k, int) and k == 0):
                    pe.wait_ge(n0_h0T, k)
                t.transpose(ps_t[:, 0:P], h0b[:, par], ident[:]).then_inc(n0_turned, 1)

            def conv(k, par):
                pe.wait_ge(n0_h0T, k + 1)
                pe.wait_ge(n0_agg, k + 1)
                if not (isinstance(k, int) and k == 0):
                    pe.wait_ge(n0_x1, k)
                t.matmul(ps_c[:, 0:D], lhsT=h0T[:, par], rhs=weight_s[:], start=True, stop=False)
                t.matmul(ps_c[:, 0:D], lhsT=aggs[:, par], rhs=weight_n[:], start=False, stop=True
                         ).then_inc(n0_conv, 1)

            def turn_norm(k, par):
                pe.wait_ge(n0_norm, k + 1)
                if not (isinstance(k, int) and k == 0):
                    pe.wait_ge(n0_h1T, k)
                t.transpose(ps_h, hnb[:, par], ident[:]).then_inc(n0_hT, 1)

            def project(k, par):
                pe.wait_ge(n0_h1T, k + 1)
                if not (isinstance(k, int) and k == 0):
                    pe.wait_ge(n0_msg, k)
                    pe.wait_ge(n0_ad, k)
                t.matmul(ps_m[:, 0:D + 1], lhsT=h1T[:, par], rhs=weight_m[:], start=True, stop=True)
                t.matmul(ps_a, lhsT=att_d_all[:], rhs=h1T[:, par], start=True, stop=True
                         ).then_inc(n0_proj, 1)

            def raw_step(i, par, first, build=True):
                free_sums(0, i)
                if not first:
                    conv(i - 2, par)
                pe.wait_ge(sel_ready, i + 1)
                for g, (j0, j1) in enumerate(GROUPS):
                    pe.wait_ge(rows_normed[g], i + 1)
                    for j in range(j0, j1):
                        last = sums(0, i, par, j)
                last.then_inc(sums_ready[0], 1)
                turn_h0(i, par)
                if not first:
                    turn_norm(i - 2, par)
                    project(i - 2, par)

            def table_step(i, par):
                free_sums(0, i)
                conv(i - 2, par)
                pe.wait_ge(sel_ready, i + 1)
                for j in range(TPB):
                    if j % 2 == 0 and not (isinstance(i, int) and i == NB - 1 and j >= LAST[0]):
                        n = 8 if j == TPB - 1 else 16
                        pe.wait_ge(gathered[par * PAIRS + j // 2], (i - par) * n + 2 * n)
                    last = sums(0, i, par, j)
                    if j == 2:
                        turn_h0(i, par)
                    if j == 7:
                        turn_norm(i - 2, par)
                    if j == 11:
                        project(i - 2, par)
                last.then_inc(sums_ready[0], 1)

            def turn_next():
                pe.wait_ge(next_ready, 1)
                for n in range(TURNS):
                    if n:
                        pe.wait_ge(next_kept, n)
                    for j in range(n * 4, min(TPB, n * 4 + 4)):
                        last = t.transpose(ps_n[:, j % 4, 0:NB], next_f[0:NB, j * P:(j + 1) * P],
                                           ident[0:NB, 0:NB])
                    last.then_inc(next_turned, 1)

            def count_bad():
                pe.wait_ge(prep, 15)
                t.matmul(ps_p[:, 0:1], lhsT=ones[:], rhs=flags1[:, 13:14], start=True, stop=True
                         ).then_inc(count1, 1)

            def pack(c, g):
                if g == 0 and not (isinstance(c, int) and c == 0):
                    pe.wait_ge(pack_kept, c)
                pe.wait_ge(hot_ready, c * 3 + (g + 1))
                skip = isinstance(c, int) and c == 0
                for s in range(*PACKS[g]):
                    if skip and s == 0:
                        continue
                    for n, u in enumerate(REACH[s][1]):
                        last = t.matmul(ps_p[:, 4 * u:4 * u + 4],
                                        lhsT=hot[:, s - PACKS[g][0], n * P:(n + 1) * P], rhs=values[:, s, :],
                                        start=(n == 0 and s == (1 if skip else 0)),
                                        stop=(s == HALO - 1), skip_group_check=True)
                last.then_inc(packed, 1)

            def pack_now(c):
                for g in range(len(PACKS)):
                    pack(c, g)

            general(0, bad)
            raw_and_table_steps(pe, raw_step, table_step, [turn_next] + [lambda: None] * 4 + [
                count_bad, lambda: pack_now(0), lambda: pack_now(1)])
            for stage in (conv, turn_norm, project):
                stage(NB - 2, 0)
                stage(NB - 1, 1)

            def self_terms(k, par):
                pe.wait_ge(h1t_in[par], (k - par) * 8 + 16)
                if not (isinstance(k, int) and k == 0):
                    pe.wait_ge(self_prod, k)
                t.matmul(ps_t[:, 0:P], lhsT=weight_m[:, 0:D], rhs=h1T[:, par], start=True, stop=True)
                t.matmul(ps_t[:, P:2 * P], lhsT=att_all[:], rhs=h1T[:, par], start=True, stop=True
                         ).then_inc(self_proj, 1)

            def gates(k, par):
                pe.wait_ge(self_added, k + 1)
                pe.wait_ge(sums_added[1], NB if isinstance(k, int) and k == NB - 1 else k + 2)
                pe.wait_ge(h1t_in[par], (k - par) * 8 + 16)
                block = agg[:, block_cols(k)]
                for g in range(2):
                    t.matmul(ps_g1[par][:, g * P:(g + 1) * P], lhsT=w_gates[:, g], rhs=block, start=True, stop=False)
                    t.matmul(ps_g1[par][:, g * P:(g + 1) * P], lhsT=w_gates[:, 3 + g], rhs=h1T[:, par],
                             start=False, stop=True)
                t.matmul(ps_g1[par][:, 2 * P:3 * P], lhsT=w_gates[:, 5], rhs=h1T[:, par], start=True, stop=True)
                t.matmul(ps_g1[par][:, 3 * P:4 * P], lhsT=w_gates[:, 2], rhs=block, start=True, stop=True
                         ).then_inc(n1_gates, 1)

            def step1(i, par, first):
                free_sums(1, i)
                if not first:
                    gates(i - 2, par)
                for g, (j0, j1) in enumerate(GROUPS1):
                    pe.wait_ge(att_ready[g], i + 1)
                    for j in range(j0, j1):
                        last = sums(1, i, par, j)
                    if g == 0 and not (isinstance(i, int) and i == 0):
                        self_terms(i - 1, 1 - par)
                    if g < 3 and not (isinstance(i, int) and i >= NB - 2):
                        pack(i + 2, g)
                last.then_inc(sums_ready[1], 1)

            bad1 = pe.value_load(bad1_i[0:1, 0:1], min_val=0, max_val=1)
            general(1, bad1)
            pairs(pe, NB, step1, last_apart=True)
            self_terms(NB - 1, 1)
            gates(NB - 2, 0)
            gates(NB - 1, 1)

            for c in range(NCH):
                pe.wait_ge(y_scaled, c + 1)
                if c >= 4:
                    pe.wait_ge(y_added, c - 3)
                for b in range(LB):
                    last = t.transpose(ps_y[c % 4][:, b * P:(b + 1) * P], y_s[c % 4][:, b, :], ident[:])
                last.then_inc(y_turned, 1)


_INS = ["x", "src", "dst", "L0_gnn_w_s", "L0_gnn_w_n", "L1_gnn_W_msg", "L1_gnn_b_msg", "L1_gnn_W_att",
        "L1_gnn_b_att", "L1_gnn_W_ih", "L1_gnn_b_ih", "L1_gnn_W_hh", "L1_gnn_b_hh", "L1_gnn_gamma",
        "L1_gnn_beta"]


def kernel(**inputs):
    import numpy as np
    import concourse.bacc as bacc
    from concourse.bass_utils import run_bass_kernel_spmd

    nc = bacc.Bacc("TRN2", target_bir_lowering=False, num_devices=1)
    arrays, args = {}, []
    for name in _INS:
        a = np.ascontiguousarray(inputs[name])
        arrays[f"in_{name}"] = a
        args.append(nc.dram_tensor(f"in_{name}", a.shape, mybir.dt.from_np(a.dtype), kind="ExternalInput").ap())
    shape = arrays["in_x"].shape
    out = nc.dram_tensor("out_0", shape, F32, kind="ExternalOutput").ap()
    gnn_program(nc, *args, out)
    r = run_bass_kernel_spmd(nc, [arrays], core_ids=[0])
    return r.results[0]["out_0"]
```
